# Optimizing a Trainium2 kernel written in Bass

```python
import numpy as np
import jax
import jax.numpy as jnp

def _softmax(x, axis=-1):
    return jax.nn.softmax(x, axis=axis)

def _gelu(x):
    return jax.nn.gelu(x, approximate=True)

def _silu(x):
    return jax.nn.silu(x)

def _sigmoid(x):
    return jax.nn.sigmoid(x)

def _layernorm(x, axis=-1, eps=1e-05):
    m = jnp.mean(x, axis=axis, keepdims=True)
    v = jnp.var(x, axis=axis, keepdims=True)
    return (x - m) / jnp.sqrt(v + eps)

def _scatter_add(tgt, idx, src, axis=0):
    return tgt.at[idx].add(src)

def _segment_sum(src, seg, n):
    return jax.ops.segment_sum(src, seg, n)
kernel_name = 'mk_rec_standalone_d1_rec_r8_9b014a'

def setup_inputs(seed: int=0):
    np.random.seed(seed)
    _w = jnp.asarray

    def _rec_inputs():
        import jax
        import jax.numpy as jnp
        _rk = jax.random.key(seed)
        r_dense_x = -0.00142785 + 1.00275 * jax.random.normal(jax.random.fold_in(_rk, 1), (2048, 13), jnp.float32)
        r_indices = jax.random.randint(jax.random.fold_in(_rk, 2), (26, 2048, 20), 0, 12500, jnp.int32)
        return (r_dense_x, r_indices)
    r_dense_x, r_indices = _rec_inputs()

    def _L0_rec_setup():
        import jax, jax.numpy as jnp
        import numpy as np
        T_TABLES, N_ROWS, M_SPA = (26, 12500, 64)
        BATCH, L_POOL = (512, 20)
        LN_BOT = [13, 512, 256, 64]
        LN_TOP = [415, 512, 256, 1]

        def _mlp_params(key, ln):
            ws, bs = ([], [])
            for i, (n, m) in enumerate(zip(ln[:-1], ln[1:])):
                kw, kb = jax.random.split(jax.random.fold_in(key, i))
                ws.append((jax.random.normal(kw, (m, n), dtype=jnp.float32) * np.sqrt(2.0 / (m + n))).astype(jnp.float32))
                bs.append((jax.random.normal(kb, (m,), dtype=jnp.float32) * np.sqrt(1.0 / m)).astype(jnp.float32))
            return (ws, bs)

        def _mlp(x, params, sigmoid_last):
            n = len(params)
            for i, (w, b) in enumerate(params):
                x = x @ w.T + b
                x = jax.nn.sigmoid(x) if sigmoid_last and i == n - 1 else jax.nn.relu(x)
            return x

        def _forward(dense_x, tables, indices, bot, top):
            x = _mlp(dense_x, bot, sigmoid_last=False)
            pooled = jax.vmap(lambda tab, ix: jnp.take(tab, ix, axis=0).sum(axis=1))(tables, indices)
            Tcat = jnp.concatenate([x[:, None, :], jnp.transpose(pooled, (1, 0, 2))], axis=1)
            Z = jnp.einsum('bim,bjm->bij', Tcat, Tcat)
            ni = T_TABLES + 1
            li, lj = jnp.tril_indices(ni, k=-1)
            R = jnp.concatenate([x, Z[:, li, lj]], axis=1)
            return _mlp(R, top, sigmoid_last=True)
        key = jax.random.key(seed)
        k_x, k_i, k_t, k_bot, k_top = jax.random.split(key, 5)
        inp = {}
        inp['dense_x'] = jax.random.normal(k_x, (BATCH, LN_BOT[0]), dtype=jnp.float32)
        inp['indices'] = jax.random.randint(k_i, (T_TABLES, BATCH, L_POOL), 0, N_ROWS, dtype=jnp.int64)
        bound = np.sqrt(1.0 / N_ROWS)
        inp['tables'] = jax.random.uniform(k_t, (T_TABLES, N_ROWS, M_SPA), dtype=jnp.float32, minval=-bound, maxval=bound)
        wb, bb = _mlp_params(k_bot, LN_BOT)
        wt, bt = _mlp_params(k_top, LN_TOP)
        for i in range(3):
            inp[f'w_bot{i}'], inp[f'b_bot{i}'] = (wb[i], bb[i])
            inp[f'w_top{i}'], inp[f'b_top{i}'] = (wt[i], bt[i])
        return inp
    _L0_rec_all = _L0_rec_setup()
    _L0_rec_in = {k: v for k, v in _L0_rec_all.items() if k in ('tables', 'w_bot0', 'b_bot0', 'w_bot1', 'b_bot1', 'w_bot2', 'b_bot2', 'w_top0', 'b_top0', 'w_top1', 'b_top1', 'w_top2', 'b_top2')}
    del _L0_rec_all
    return {'r_dense_x': r_dense_x, 'r_indices': r_indices, 'L0_rec_tables': _L0_rec_in['tables'], 'L0_rec_w_bot0': _L0_rec_in['w_bot0'], 'L0_rec_b_bot0': _L0_rec_in['b_bot0'], 'L0_rec_w_bot1': _L0_rec_in['w_bot1'], 'L0_rec_b_bot1': _L0_rec_in['b_bot1'], 'L0_rec_w_bot2': _L0_rec_in['w_bot2'], 'L0_rec_b_bot2': _L0_rec_in['b_bot2'], 'L0_rec_w_top0': _L0_rec_in['w_top0'], 'L0_rec_b_top0': _L0_rec_in['b_top0'], 'L0_rec_w_top1': _L0_rec_in['w_top1'], 'L0_rec_b_top1': _L0_rec_in['b_top1'], 'L0_rec_w_top2': _L0_rec_in['w_top2'], 'L0_rec_b_top2': _L0_rec_in['b_top2']}

def reference(r_dense_x, r_indices, L0_rec_tables, L0_rec_w_bot0, L0_rec_b_bot0, L0_rec_w_bot1, L0_rec_b_bot1, L0_rec_w_bot2, L0_rec_b_bot2, L0_rec_w_top0, L0_rec_b_top0, L0_rec_w_top1, L0_rec_b_top1, L0_rec_w_top2, L0_rec_b_top2):
    import jax
    import jax.numpy as jnp

    def _L0_rec_ref(dense_x, indices, tables, w_bot0, b_bot0, w_bot1, b_bot1, w_bot2, b_bot2, w_top0, b_top0, w_top1, b_top1, w_top2, b_top2):
        import jax, jax.numpy as jnp
        import numpy as np
        T_TABLES, N_ROWS, M_SPA = (26, 12500, 64)
        BATCH, L_POOL = (512, 20)
        LN_BOT = [13, 512, 256, 64]
        LN_TOP = [415, 512, 256, 1]

        def _mlp_params(key, ln):
            ws, bs = ([], [])
            for i, (n, m) in enumerate(zip(ln[:-1], ln[1:])):
                kw, kb = jax.random.split(jax.random.fold_in(key, i))
                ws.append((jax.random.normal(kw, (m, n), dtype=jnp.float32) * np.sqrt(2.0 / (m + n))).astype(jnp.float32))
                bs.append((jax.random.normal(kb, (m,), dtype=jnp.float32) * np.sqrt(1.0 / m)).astype(jnp.float32))
            return (ws, bs)

        def _mlp(x, params, sigmoid_last):
            n = len(params)
            for i, (w, b) in enumerate(params):
                x = x @ w.T + b
                x = jax.nn.sigmoid(x) if sigmoid_last and i == n - 1 else jax.nn.relu(x)
            return x

        def _forward(dense_x, tables, indices, bot, top):
            x = _mlp(dense_x, bot, sigmoid_last=False)
            pooled = jax.vmap(lambda tab, ix: jnp.take(tab, ix, axis=0).sum(axis=1))(tables, indices)
            Tcat = jnp.concatenate([x[:, None, :], jnp.transpose(pooled, (1, 0, 2))], axis=1)
            Z = jnp.einsum('bim,bjm->bij', Tcat, Tcat)
            ni = T_TABLES + 1
            li, lj = jnp.tril_indices(ni, k=-1)
            R = jnp.concatenate([x, Z[:, li, lj]], axis=1)
            return _mlp(R, top, sigmoid_last=True)
        bot = [(w_bot0, b_bot0), (w_bot1, b_bot1), (w_bot2, b_bot2)]
        top = [(w_top0, b_top0), (w_top1, b_top1), (w_top2, b_top2)]
        return _forward(dense_x, tables, indices, bot, top)
    y = _L0_rec_ref(r_dense_x, r_indices, L0_rec_tables, L0_rec_w_bot0, L0_rec_b_bot0, L0_rec_w_bot1, L0_rec_b_bot1, L0_rec_w_bot2, L0_rec_b_bot2, L0_rec_w_top0, L0_rec_b_top0, L0_rec_w_top1, L0_rec_b_top1, L0_rec_w_top2, L0_rec_b_top2)
    return y

_drawn_inputs = setup_inputs


def setup_inputs(seed=0):
    import zlib

    import numpy as np

    out = dict(_drawn_inputs(seed))
    spreads = {}
    factors = {'r_dense_x': 8.0,
     'L0_rec_tables': 8.0,
     'L0_rec_w_bot0': 8.0,
     'L0_rec_b_bot0': 8.0,
     'L0_rec_w_bot1': 8.0,
     'L0_rec_b_bot1': 8.0,
     'L0_rec_w_bot2': 8.0,
     'L0_rec_b_bot2': 6.787,
     'L0_rec_w_top0': 4.116,
     'L0_rec_b_top0': 54.224,
     'L0_rec_w_top1': 5.197,
     'L0_rec_b_top1': 200.0}
    for name, (base, spread) in spreads.items():
        noise = np.random.default_rng([zlib.crc32(name.encode()), seed]).standard_normal(out[name].shape)
        drawn = base * np.exp(spread * noise) if base else spread * noise
        out[name] = jnp.asarray(drawn.astype(out[name].dtype))
    for name, factor in factors.items():
        out[name] = (out[name] * factor).astype(out[name].dtype)
    return out
```

```python
from contextlib import ExitStack

import concourse.bass as bass
from concourse import mybir

ALU = mybir.AluOpType
ACT = mybir.ActivationFunctionType
AX = mybir.AxisListType
F32 = mybir.dt.float32
F16 = mybir.dt.float16
BF16 = mybir.dt.bfloat16
I32 = mybir.dt.int32
F8 = mybir.dt.float8e3

P = 128
QUAD = 32
BANK = 512

ROUND = 1.5 * 2.0 ** 23
HI_EXP = 14
LO_SHIFT = 11
COUNT_UNIT = 2.0 ** 6
EXP_UNIT = 2 ** 23
EXP_MASK = 0x7F800000
TINY = 2.0 ** -100
ABSENT = 1 << 20


def build(nc, dense_x, indices, tables, w_bot, b_bot, w_top, b_top, out):
    T, B, L = indices.shape
    _, ROWS, D = tables.shape
    SLOTS = T + 1

    SPAN = -(-ROWS // P)
    COLS = -(-SPAN // 3)
    SHIFT = SPAN * P - ROWS
    GS = P // L
    GK = GS * L
    GC = GS * COLS
    NB = BANK
    BLOCKS = B // NB
    GROUPS = -(-NB // GS)
    TAIL = NB - (GROUPS - 1) * GS
    UG = 4
    UNITS = -(-GROUPS // UG)
    BPAD = GROUPS * GS
    CHUNKS = 7
    CJ = SPAN // CHUNKS
    assert B % NB == 0 and UNITS % 2 == 0 and BLOCKS % 2 == 0 and SPAN % CHUNKS == 0
    assert 2 * GC <= BANK and L < 32 and GROUPS <= P and 2 * D == P and SLOTS <= QUAD

    NBOT = [dense_x.shape[1]] + [w.shape[0] for w in w_bot]
    NTOP = [w_top[0].shape[1]] + [w.shape[0] for w in w_top]
    NF = NTOP[0]
    FCH = -(-NF // P)
    CHUNK_B = B // NB
    PAIR_ROW = [D + i * (i - 1) // 2 for i in range(SLOTS)]
    assert NF == PAIR_ROW[-1] + SLOTS - 1 and NTOP[3] == 1 and NBOT[3] == D

    rows_flat = tables.rearrange("t n d -> (t n) d")
    pooled_dram = nc.dram_tensor("pooled", [SLOTS, D, B], F32, kind="Internal").ap()

    def units_of(u):
        return range(u * UG, min((u + 1) * UG, GROUPS))

    ctx = ExitStack()
    with ctx:
        def sem(name):
            return ctx.enter_context(nc.semaphore(name))

        weights_in = sem("weights_in")
        consts_ready = sem("consts_ready")
        const_step = sem("const_step")
        turned = sem("turned")
        unturned = sem("unturned")
        bot_mm = sem("bot_mm")
        bot_act = sem("bot_act")
        bot_stored = sem("bot_stored")
        table_loaded = sem("table_loaded")
        idx_loaded = sem("idx_loaded")
        idx_converted = sem("idx_converted")
        idx_turned = sem("idx_turned")
        idx_copied = sem("idx_copied")
        idx_step = sem("idx_step")
        idx_ready = sem("idx_ready")
        idx_adopted = sem("idx_adopted")
        rowmax_part = sem("rowmax_part")
        rowmax_ready = sem("rowmax_ready")
        tabmax_ready = sem("tabmax_ready")
        scale_step = sem("scale_step")
        scale_ready = sem("scale_ready")
        coef_adopted = sem("coef_adopted")
        scaled = sem("scaled")
        hi_ready = sem("hi_ready")
        diff_ready = sem("diff_ready")
        parts_ready = sem("parts_ready")
        pool_waited = sem("pool_waited")
        chunk_used = sem("chunk_used")
        onehots_ready = sem("onehots_ready")
        unit_counted = sem("unit_counted")
        counts_ready = sem("counts_ready")
        block_summed = sem("block_summed")
        acc_free = sem("acc_free")
        lo_taken = sem("lo_taken")
        pooled_ready = sem("pooled_ready")
        pooled_stored = sem("pooled_stored")
        pooled_free = sem("pooled_free")
        slots_in = [sem(f"slots_in{i}") for i in range(2)]
        pads_zeroed = sem("pads_zeroed")
        dense_in = sem("dense_in")
        grams_ready = sem("grams_ready")
        diag_act = sem("diag_act")
        diag_dve = sem("diag_dve")
        pairs_in = sem("pairs_in")
        top_mm = sem("top_mm")
        top_act = sem("top_act")
        out_stored = sem("out_stored")

        def sb(stack, name, shape, dt):
            return stack.enter_context(nc.sbuf_tensor(name, shape, dt))

        ident = sb(ctx, "ident", [P, P], F32)
        iota_cols = sb(ctx, "iota_cols", [P, GC], BF16)
        sample_base = sb(ctx, "sample_base", [P, 1], F32)
        w_top0T = sb(ctx, "w_top0T", [P, FCH, NTOP[1]], F32)
        w_top1T = sb(ctx, "w_top1T", [P, NTOP[1] // P, NTOP[2]], F32)
        w_top2T = sb(ctx, "w_top2T", [P, NTOP[2] // P], F32)
        b_top0c = sb(ctx, "b_top0c", [P, NTOP[1] // P], F32)
        b_top1c = sb(ctx, "b_top1c", [P, NTOP[2] // P], F32)
        b_top2c = sb(ctx, "b_top2c", [1, 1], F32)
        idx_raw = sb(ctx, "idx_raw", [GROUPS, BLOCKS, GK], I32)

        early = ExitStack()
        w_bot0r = sb(early, "w_bot0r", [P, NBOT[1] // P, NBOT[0]], F32)
        w_bot1r = sb(early, "w_bot1r", [P, NBOT[2] // P, NBOT[1]], F32)
        w_bot2r = sb(early, "w_bot2r", [D, NBOT[2]], F32)
        w_top0r = sb(early, "w_top0r", [P, NTOP[1] // P, NF], F32)
        w_top1r = sb(early, "w_top1r", [P, NTOP[2] // P, NTOP[1]], F32)
        xr = sb(early, "xr", [P, B // P, NBOT[0]], F32)
        xT = sb(early, "xT", [NBOT[0], B], F32)
        w_bot0T = sb(early, "w_bot0T", [NBOT[0], NBOT[1]], F32)
        w_bot1T = sb(early, "w_bot1T", [P, NBOT[1] // P, NBOT[2]], F32)
        w_bot2T = sb(early, "w_bot2T", [P, NBOT[2] // P, D], F32)
        b_bot0c = sb(early, "b_bot0c", [P, NBOT[1] // P], F32)
        b_bot1c = sb(early, "b_bot1c", [P, NBOT[2] // P], F32)
        b_bot2c = sb(early, "b_bot2c", [D, 1], F32)
        h_bot0 = sb(early, "h_bot0", [P, NBOT[1] // P, B], F32)
        h_bot1 = sb(early, "h_bot1", [P, NBOT[2] // P, B], F32)
        x_bot = sb(early, "x_bot", [D, B], F32)
        iota_i = sb(early, "iota_i", [P, 1], F32)
        early.close()

        loop = ExitStack()
        counts = [sb(loop, f"counts{i}", [P, COLS, BPAD], I32) for i in range(2)]
        count_bytes = [c[:, :, :].rearrange("p c b -> p (c b)").bitcast(F8).rearrange(
            "p (c b f) -> p c b f", b=BPAD, f=4) for c in counts]
        raw = sb(loop, "raw", [P, SPAN, D], F32)
        parts = sb(loop, "parts", [P, SPAN, 2 * D], F16)
        onehot_p = sb(loop, "onehot_p", [GK, 2 * UG, P], BF16)
        onehot_c = sb(loop, "onehot_c", [GK, 2 * UG, GC], BF16)
        idx_f = sb(loop, "idx_f", [GROUPS, BLOCKS, GK], F32)
        NI = BLOCKS * GROUPS
        idx_t = sb(loop, "idx_t", [GK, NI], F32)
        scratch = sb(loop, "scratch", [GK, NI], F32)
        place_next = sb(loop, "place_next", [GK, 3, NI], F32)
        place = sb(loop, "place", [GK, 3, NI], F32)
        rowmax = sb(loop, "rowmax", [P, CHUNKS + 2], F32)
        scale_tmp = sb(loop, "scale_tmp", [P, 4], F32)
        coef_next = sb(loop, "coef_next", [P, 3], F32)
        coef = sb(loop, "coef", [P, 2], F32)
        lo_sum = sb(loop, "lo_sum", [D, NB], F32)
        pooled = sb(loop, "pooled_sb", [D, 2, NB], F32)
        loop.close()

        late = ExitStack()
        HG = 64
        TILES = NB // (2 * HG)
        slots = [sb(late, f"slots{i}", [P, CHUNK_B, QUAD, HG], F32) for i in range(2)]
        zt = sb(late, "zt", [P, SLOTS, NB], F32)
        feats = sb(late, "feats", [P, FCH, B], F32)
        late.close()
        final = ExitStack()
        sb(final, "_skip", [P, 2 * QUAD * CHUNK_B * HG * 0 + 1], F32)
        h_top0 = sb(final, "h_top0", [P, NTOP[1] // P, B], F32)
        h_top1 = sb(final, "h_top1", [P, NTOP[2] // P, B], F32)
        y = sb(final, "y", [1, B], F32)
        final.close()

        unit_ps = [ctx.enter_context(nc.psum_tensor(f"unit_ps{i}", [P, UG, BANK // 2], F32)) for i in range(2)]
        acc = [ctx.enter_context(nc.psum_tensor(f"acc{i}", [P, BANK], F32)) for i in range(2)]
        idx_ps = ctx.enter_context(nc.psum_tensor("idx_ps", [P, BANK], F32))
        spare = ctx.enter_context(nc.psum_tensor("spare", [P, BANK], F32))
        banks = [unit_ps[i][:, 2 * j:2 * j + 2, :].rearrange("p a b -> p (a b)") for i in range(2) for j in range(2)]
        banks += [acc[0][:, :], acc[1][:, :], idx_ps[:, :], spare[:, :]]

        block = ctx.enter_context(nc.Block())

        turns = []
        for m in range(B // P):
            turns.append((xr[:, m, :], xT[:, m * P:(m + 1) * P]))
        for m in range(NBOT[1] // P):
            turns.append((w_bot0r[:, m, :], w_bot0T[:, m * P:(m + 1) * P]))
        for m in range(NBOT[2] // P):
            for k in range(NBOT[1] // P):
                turns.append((w_bot1r[:, m, k * P:(k + 1) * P], w_bot1T[:, k, m * P:(m + 1) * P]))
        for k in range(NBOT[2] // P):
            turns.append((w_bot2r[:, k * P:(k + 1) * P], w_bot2T[:, k, :]))
        for m in range(NTOP[1] // P):
            for k in range(FCH):
                n = min(P, NF - k * P)
                turns.append((w_top0r[:, m, k * P:k * P + n], w_top0T[0:n, k, m * P:(m + 1) * P]))
        for m in range(NTOP[2] // P):
            for k in range(NTOP[1] // P):
                turns.append((w_top1r[:, m, k * P:(k + 1) * P], w_top1T[:, k, m * P:(m + 1) * P]))

        weight_loads = [
            (xr[:, :, :], dense_x.rearrange("(m p) k -> p m k", p=P)),
            (w_bot0r[:, :, :], w_bot[0].rearrange("(m p) k -> p m k", p=P)),
            (w_bot1r[:, :, :], w_bot[1].rearrange("(m p) k -> p m k", p=P)),
            (w_bot2r[:, :], w_bot[2]),
            (w_top0r[:, :, :], w_top[0].rearrange("(m p) k -> p m k", p=P)),
            (w_top1r[:, :, :], w_top[1].rearrange("(m p) k -> p m k", p=P)),
            (w_top2T[:, :], w_top[2].rearrange("a (m p) -> p (a m)", p=P)),
            (b_bot0c[:, :], b_bot[0].rearrange("(m p) -> p m", p=P)),
            (b_bot1c[:, :], b_bot[1].rearrange("(m p) -> p m", p=P)),
            (b_bot2c[:, :], b_bot[2].rearrange("(m p) -> p m", p=D)),
            (b_top0c[:, :], b_top[0].rearrange("(m p) -> p m", p=P)),
            (b_top1c[:, :], b_top[1].rearrange("(m p) -> p m", p=P)),
            (b_top2c[:, :], b_top[2].rearrange("(m p) -> p m", p=1)),
        ]

        def layer(K, M, wT, src):
            for n in range(B // NB):
                for m in range(-(-M // P)):
                    mm = min(P, M - m * P)
                    terms = []
                    for k in range(-(-K // P)):
                        kk = min(P, K - k * P)
                        terms.append((wT(k, kk, m, mm), src(k, kk, n)))
                    yield m, mm, n, terms

        bot_layers = [
            list(layer(NBOT[0], NBOT[1], lambda k, kk, m, mm: w_bot0T[:, m * P:m * P + mm],
                       lambda k, kk, n: xT[:, n * NB:(n + 1) * NB])),
            list(layer(NBOT[1], NBOT[2], lambda k, kk, m, mm: w_bot1T[:, k, m * P:m * P + mm],
                       lambda k, kk, n: h_bot0[:, k, n * NB:(n + 1) * NB])),
            list(layer(NBOT[2], NBOT[3], lambda k, kk, m, mm: w_bot2T[:, k, :],
                       lambda k, kk, n: h_bot1[:, k, n * NB:(n + 1) * NB])),
        ]
        top_layers = [
            list(layer(NF, NTOP[1], lambda k, kk, m, mm: w_top0T[0:kk, k, m * P:m * P + mm],
                       lambda k, kk, n: feats[0:kk, k, n * NB:(n + 1) * NB])),
            list(layer(NTOP[1], NTOP[2], lambda k, kk, m, mm: w_top1T[:, k, m * P:m * P + mm],
                       lambda k, kk, n: h_top0[:, k, n * NB:(n + 1) * NB])),
            list(layer(NTOP[2], 1, lambda k, kk, m, mm: w_top2T[:, k:k + 1],
                       lambda k, kk, n: h_top1[:, k, n * NB:(n + 1) * NB])),
        ]
        bot_tiles = [(l, *t) for l, tiles in enumerate(bot_layers) for t in tiles]
        top_tiles = [(l, *t) for l, tiles in enumerate(top_layers) for t in tiles]
        mlp_banks = banks[4:8]

        def needed(tiles, i):
            l, n = tiles[i][0], tiles[i][3]
            done = [j for j, t in enumerate(tiles) if t[0] == l - 1 and t[3] == n]
            return done[-1] + 1 if done else 0

        def pieces(i):
            at, j = PAIR_ROW[i], 0
            while j < i:
                n = min(i - j, P - (at + j) % P)
                yield j, n, (at + j) // P, (at + j) % P
                j += n

        NPIECE = sum(1 for i in range(1, SLOTS) for _ in pieces(i))
        GRAMS_PER_BANK = 4
        NBANKS = NB // GRAMS_PER_BANK
        BANKS_PER_TILE = NBANKS // TILES
        HALF_BANKS = BANKS_PER_TILE // 2

        PER_UNIT = 4

        def take_diagonals(eng, copy, b, quarters, done):
            r, half, w = b // BANKS_PER_TILE, b % 2, b % BANKS_PER_TILE // 2
            g0 = r * 2 * HG + half * HG + GRAMS_PER_BANK * w
            eng.wait_ge(grams_ready, b + 1)
            for k in quarters:
                rows = slice(QUAD * k, QUAD * (k + 1))
                src = banks[b % 4].rearrange("p (x k s) -> p x k s", x=GRAMS_PER_BANK, k=CHUNK_B)
                last = copy(zt[rows, :, g0:g0 + GRAMS_PER_BANK].rearrange("p s x -> p x s"),
                            src[rows, :, k, 0:SLOTS])
            last.then_inc(done, 1)

        @block.sync
        def _(sp):
            def load_table(src):
                sp.dma_start(raw[:, :, :], src.rearrange("(p j) d -> p j d", p=P)).then_inc(table_loaded, 16)

            def load_indices(t):
                flat = indices[t].rearrange("b l -> (b l)").rearrange("(k r) -> k r", k=BLOCKS)
                cut = (GROUPS - 1) * GK
                sp.dma_start(idx_raw[0:GROUPS - 1, :, :],
                             flat[:, 0:cut].rearrange("k (g r) -> g k r", r=GK)).then_inc(idx_loaded, 16)
                sp.dma_start(idx_raw[GROUPS - 1:GROUPS, :, 0:TAIL * L],
                             flat[:, cut:NB * L].rearrange("k (g r) -> g k r", g=1)).then_inc(idx_loaded, 16)

            def store_pooled(t, k):
                sp.wait_ge(pooled_ready, BLOCKS * t + k + 1)
                sp.dma_start(pooled_dram[t + 1, :, k * NB:(k + 1) * NB],
                             pooled[:, k % 2, :]).then_inc(pooled_stored, 16)
                sp.wait_ge(pooled_stored, 16 * (BLOCKS * t + k + 1))
                sp.sem_inc(pooled_free, 1)

            sp.sem_inc(pooled_free, 2)
            for dst, src in weight_loads:
                with nc.allow_non_contiguous_dma(reason="small weights and biases"):
                    sp.dma_start(dst, src).then_inc(weights_in, 16)
            sp.wait_ge(const_step, 3)
            load_indices(0)
            sp.wait_ge(bot_stored, 16)
            load_table(rows_flat[0:SPAN * P, :])
            with sp.Fori(0, T - 2) as t:
                sp.wait_ge(idx_converted, t + 1)
                load_indices(t + 1)
                sp.wait_ge(parts_ready, CHUNKS * t + CHUNKS)
                load_table(rows_flat[bass.ds((t + 1) * ROWS, SPAN * P), :])
                for k in range(BLOCKS):
                    store_pooled(t, k)
            t = T - 2
            sp.wait_ge(idx_converted, t + 1)
            load_indices(t + 1)
            sp.wait_ge(parts_ready, CHUNKS * t + CHUNKS)
            load_table(rows_flat[(t + 1) * ROWS - SHIFT:(t + 2) * ROWS, :])
            for k in range(BLOCKS):
                store_pooled(t, k)
            for k in range(BLOCKS):
                store_pooled(T - 1, k)

            sp.dma_start(feats[0:D, 0, :], pooled_dram[0, :, :]).then_inc(dense_in, 16)
            sp.wait_ge(pads_zeroed, 2)
            for r in range(TILES):
                if r >= 2:
                    sp.wait_ge(grams_ready, BANKS_PER_TILE * (r - 1))
                for half in range(2):
                    g0 = r * 2 * HG + half * HG
                    src = pooled_dram.rearrange("s d (k g) -> d s k g", g=NB)
                    for s in range(SLOTS):
                        sp.dma_start(slots[r % 2][half * D:(half + 1) * D, :, s, :],
                                     src[:, s, :, g0:g0 + HG]).then_inc(slots_in[r % 2], 16)
            sp.wait_ge(diag_act, NBANKS)
            sp.wait_ge(diag_dve, NBANKS)
            for i in range(1, SLOTS):
                for j, n, ch, p0 in pieces(i):
                    for k in range(CHUNK_B):
                        sp.dma_start(feats[p0:p0 + n, ch, k * NB:(k + 1) * NB],
                                     zt[QUAD * k + j:QUAD * k + j + n, i, :]).then_inc(pairs_in, 16)
            sp.wait_ge(top_act, len(top_tiles))
            sp.dma_start(out.rearrange("b a -> a b"), y[:, :]).then_inc(out_stored, 16)
            sp.wait_ge(out_stored, 16)

        @block.gpsimd
        def _(pool):
            def await_alone(semaphore, value):
                pool.wait_ge(semaphore, value)
                pool.sem_inc(pool_waited, 1)

            nc.gpsimd.memset(ident[:, :], 0.0).then_inc(const_step, 1)
            nc.gpsimd.iota(iota_cols[:, :], pattern=[[1, GC]], base=0, channel_multiplier=0,
                           allow_small_or_imprecise_dtypes=True).then_inc(consts_ready, 1)
            nc.gpsimd.iota(iota_i[:, :], pattern=[[0, 1]], base=0, channel_multiplier=1,
                           allow_small_or_imprecise_dtypes=True).then_inc(const_step, 1)
            nc.gpsimd.memset(idx_raw[:, :, :], ABSENT).then_inc(const_step, 1)
            pool.wait_ge(const_step, 3)
            nc.gpsimd.affine_select(out=ident[:, :], in_=ident[:, :], compare_op=ALU.not_equal, fill=1.0,
                                    base=0, pattern=[[-1, P]], channel_multiplier=1).then_inc(consts_ready, 1)
            nc.gpsimd.tensor_scalar(iota_i[:, :], iota_i[:, :], -(L - 1) / 2, 1.0 / L,
                                    ALU.add, ALU.mult).then_inc(const_step, 1)
            pool.wait_ge(const_step, 4)
            nc.gpsimd.tensor_scalar(sample_base[:, :], iota_i[:, :], ROUND, -ROUND,
                                    ALU.add, ALU.add).then_inc(consts_ready, 1)
            pool.wait_ge(consts_ready, 3)

            STEPS = 8
            part_i, col_i, weight_i = (place_next[:, i, :] for i in range(3))

            def convert_indices(t, shift):
                await_alone(idx_loaded, 32 * t + 32)
                nc.gpsimd.tensor_scalar(idx_f[:, :, :], idx_raw[:, :, :], float(shift), None,
                                        ALU.add).then_inc(idx_converted, 1)

            def place_indices(t, first=False):
                n = [0]

                def step(ins):
                    n[0] += 1
                    ins.then_inc(idx_step, 1)
                    await_alone(idx_step, STEPS * t + n[0])

                pool.wait_ge(idx_copied, t + 1)
                if not first:
                    pool.wait_ge(idx_adopted, t)
                pool.sem_inc(pool_waited, 1)
                ts, tt = nc.gpsimd.tensor_scalar, nc.gpsimd.tensor_tensor
                step(ts(scratch[:, :], idx_t[:, :], -(SPAN - 1) / 2, 1.0 / SPAN, ALU.add, ALU.mult))
                step(ts(part_i, scratch[:, :], ROUND, -ROUND, ALU.add, ALU.add))
                step(ts(scratch[:, :], part_i, -float(SPAN), 0.0, ALU.mult, ALU.add))
                step(tt(idx_t[:, :], idx_t[:, :], scratch[:, :], ALU.add))
                step(ts(scratch[:, :], idx_t[:, :], -(COLS - 1) / 2, 1.0 / COLS, ALU.add, ALU.mult))
                step(ts(scratch[:, :], scratch[:, :], ROUND, -ROUND, ALU.add, ALU.add))
                step(ts(weight_i.bitcast(I32), scratch[:, :], 8.0 * EXP_UNIT, 127.0 * EXP_UNIT, ALU.mult, ALU.add))
                step(ts(scratch[:, :], scratch[:, :], -float(COLS), 0.0, ALU.mult, ALU.add))
                assert n[0] == STEPS
                nc.gpsimd.tensor_tensor(idx_t[:, :], idx_t[:, :], scratch[:, :], ALU.add).then_inc(idx_ready, 1)
                await_alone(idx_ready, 2 * t + 1)
                nc.gpsimd.tensor_scalar(col_i, idx_t[:, :], float(GS), sample_base[0:GK, :], ALU.mult,
                                        ALU.add).then_inc(idx_ready, 1)

            def table_max(t):
                await_alone(rowmax_ready, t + 1)
                nc.gpsimd.partition_all_reduce(rowmax[:, CHUNKS + 1:CHUNKS + 2], rowmax[:, CHUNKS:CHUNKS + 1], P,
                                               bass.bass_isa.ReduceOp.max).then_inc(tabmax_ready, 1)

            def make_lo(t, q):
                c = slice(q * CJ, (q + 1) * CJ)
                pool.wait_ge(hi_ready, CHUNKS * t + q + 1)
                nc.gpsimd.tensor_tensor(raw[:, c, :], raw[:, c, :], parts[:, c, 0:D],
                                        ALU.subtract).then_inc(diff_ready, 1)
                await_alone(diff_ready, CHUNKS * t + q + 1)
                nc.gpsimd.tensor_scalar(parts[:, c, D:2 * D], raw[:, c, :], 2.0 ** LO_SHIFT, 0.0, ALU.mult,
                                        ALU.add).then_inc(parts_ready, 1)

            def prepare(t, shift, first=False):
                convert_indices(t, shift)
                place_indices(t, first)
                table_max(t)
                for q in range(CHUNKS):
                    make_lo(t, q)

            pool.wait_ge(bot_stored, 16)
            prepare(0, 0, first=True)
            with pool.Fori(0, T - 2) as t:
                prepare(t + 1, 0)
            prepare(T - 1, SHIFT)
            pool.wait_ge(block_summed, BLOCKS * T)
            for q in range(2):
                nc.gpsimd.memset(slots[q][:, :, SLOTS:QUAD, :], 0.0).then_inc(pads_zeroed, 1)

        @block.tensor
        def _(pe):
            pe.wait_ge(consts_ready, 2)
            pe.wait_ge(weights_in, 16 * len(weight_loads))
            for i, (src, dst) in enumerate(turns):
                if i >= 4 * 4 and i % 4 == 0:
                    pe.wait_ge(unturned, i // 4 - 3)
                kp, m = src.shape[0], src.shape[1]
                last = nc.tensor.transpose(banks[i // 4 % 4][0:m, i % 4 * P:i % 4 * P + kp], src,
                                           ident[0:kp, 0:kp])
                if i % 4 == 3 or i == len(turns) - 1:
                    last.then_inc(turned, 1)

            def mlp(tiles, mm_sem, act_sem):
                for i, (l, m, mm, n, terms) in enumerate(tiles):
                    ready = max(needed(tiles, i), i - 3)
                    if ready > 0:
                        pe.wait_ge(act_sem, ready)
                    for k, (w, x) in enumerate(terms):
                        last = nc.tensor.matmul(mlp_banks[i % 4][0:mm, :], w, x, start=(k == 0),
                                                stop=(k == len(terms) - 1))
                    last.then_inc(mm_sem, 1)

            pe.wait_ge(unturned, -(-len(turns) // 4))
            mlp(bot_tiles, bot_mm, bot_act)

            def turn_indices(t, first=False):
                pe.wait_ge(idx_converted, t + 1)
                if not first:
                    pe.wait_ge(idx_copied, t)
                for k in range(BLOCKS):
                    last = nc.tensor.transpose(idx_ps[0:GK, k * GROUPS:(k + 1) * GROUPS], idx_f[:, k, :],
                                               ident[0:GROUPS, 0:GROUPS])
                last.then_inc(idx_turned, 1)

            def count_unit(t, k, u, first=False):
                n = UNITS * (BLOCKS * t + k) + u
                pe.wait_ge(onehots_ready, n + 1)
                if not (first and u < 2):
                    pe.wait_ge(counts_ready, n - 1)
                for g in units_of(u):
                    s, r = g % UG, UG * (u % 2) + g % UG
                    last = nc.tensor.matmul(unit_ps[u % 2][:, s, 0:GC], onehot_p[:, r, :], onehot_c[:, r, :],
                                            start=True, stop=True)
                last.then_inc(unit_counted, 1)

            def await_rows(t, k, j0, j1):
                n = BLOCKS * t + k
                if j0 == 0:
                    pe.wait_ge(counts_ready, UNITS * n + UNITS)
                    pe.wait_ge(acc_free, n + 1)
                for j in range(j0, j1):
                    if k == 0 and j % CJ == 0:
                        pe.wait_ge(parts_ready, CHUNKS * t + j // CJ + 1)

            def sum_rows(t, k, j):
                mm = nc.tensor.matmul(acc[k % 2][:, 0:NB], parts[:, j, :],
                                      count_bytes[k % 2][:, j % COLS, 0:NB, j // COLS],
                                      start=(j == 0), stop=(j == SPAN - 1))
                if j == SPAN - 1:
                    mm.then_inc(block_summed, 1)
                elif k == BLOCKS - 1 and j % CJ == CJ - 1:
                    mm.then_inc(chunk_used, 1)

            def phase(t, k, tn, kn):
                for u in range(UNITS):
                    j1 = SPAN if u == UNITS - 1 else PER_UNIT * (u + 1)
                    await_rows(t, k, PER_UNIT * u, j1)
                    count_unit(tn, kn, u)
                    for j in range(PER_UNIT * u, PER_UNIT * (u + 1)):
                        sum_rows(t, k, j)
                for j in range(PER_UNIT * UNITS, SPAN):
                    sum_rows(t, k, j)

            turn_indices(0, first=True)
            for u in range(UNITS):
                count_unit(0, 0, u, first=True)

            with pe.Fori(0, T - 1) as t:
                phase(t, 0, t, 1)
                turn_indices(t + 1)
                phase(t, 1, t, 2)
                phase(t, 2, t, 3)
                phase(t, 3, t + 1, 0)
            for k in range(BLOCKS - 1):
                phase(T - 1, k, T - 1, k + 1)
            await_rows(T - 1, BLOCKS - 1, 0, SPAN)
            for j in range(SPAN):
                sum_rows(T - 1, BLOCKS - 1, j)

            pe.wait_ge(acc_free, BLOCKS * T + 2)
            for b in range(NBANKS):
                r, half, w = b // BANKS_PER_TILE, b % 2, b % BANKS_PER_TILE // 2
                if b % BANKS_PER_TILE == 0:
                    pe.wait_ge(slots_in[r % 2], 32 * SLOTS * (r // 2 + 1))
                    pe.wait_ge(pads_zeroed, 2)
                if b >= 4:
                    pe.wait_ge(diag_act, b - 3)
                    pe.wait_ge(diag_dve, b - 3)
                tile = slots[r % 2][half * D:(half + 1) * D, :, :, :].rearrange("p k s g -> p g (k s)")
                for x in range(GRAMS_PER_BANK):
                    g = GRAMS_PER_BANK * w + x
                    last = nc.tensor.matmul(banks[b % 4][:, x * P:(x + 1) * P], tile[:, g, :],
                                            tile[:, g, :], start=True, stop=True)
                last.then_inc(grams_ready, 1)

            pe.wait_ge(pairs_in, 16 * NPIECE * CHUNK_B)
            pe.wait_ge(dense_in, 16)
            mlp(top_tiles, top_mm, top_act)

        @block.scalar
        def _(act):
            def activated(l, m, n, outs, biases):
                cols = slice(n * NB, (n + 1) * NB)
                return (outs[l][:, m, cols] if l < 2 else outs[l][:, cols]), biases[l][:, m:m + 1]

            for i, (l, m, mm, n, terms) in enumerate(bot_tiles):
                act.wait_ge(bot_mm, i + 1)
                dst, bias = activated(l, m, n, (h_bot0, h_bot1, x_bot), (b_bot0c, b_bot1c, b_bot2c))
                nc.scalar.activation(dst, mlp_banks[i % 4][0:mm, :], ACT.Relu, bias=bias).then_inc(bot_act, 1)
            act.wait_ge(bot_act, len(bot_tiles))
            act.dma_start(pooled_dram[0, :, :], x_bot[:, :]).then_inc(bot_stored, 16)
            act.wait_ge(bot_stored, 16)

            def scale_chunk(t, q):
                c = slice(q * CJ, (q + 1) * CJ)
                if q == 0:
                    act.wait_ge(scale_ready, t + 1)
                nc.scalar.activation(raw[:, c, :], raw[:, c, :], ACT.Copy,
                                     scale=coef_next[:, 2:3]).then_inc(scaled, 1)

            def make_hi(t, q, first=False):
                c = slice(q * CJ, (q + 1) * CJ)
                act.wait_ge(scaled, CHUNKS * t + q + 1)
                if not first:
                    if q == CHUNKS - 1:
                        act.wait_ge(block_summed, BLOCKS * t)
                    else:
                        act.wait_ge(chunk_used, (CHUNKS - 1) * (t - 1) + q + 1)
                nc.scalar.copy(parts[:, c, 0:D], raw[:, c, :]).then_inc(hi_ready, 1)

            def unpack_unit(t, k, u, first=False):
                n = UNITS * (BLOCKS * t + k) + u
                act.wait_ge(unit_counted, n + 1)
                g = len(units_of(u))
                nc.scalar.copy(
                    counts[k % 2][:, :, u * UG * GS:(u * UG + g) * GS].rearrange("p c (g s) -> p g c s", s=GS),
                    unit_ps[u % 2][:, 0:g, 0:GC].rearrange("p g (c s) -> p g c s", s=GS),
                ).then_inc(counts_ready, 1)

            for q in range(CHUNKS):
                scale_chunk(0, q)
            for q in range(CHUNKS):
                make_hi(0, q, first=True)
            for u in range(UNITS):
                unpack_unit(0, 0, u, first=True)
            with act.Fori(0, T - 1) as t:
                for k in range(1, BLOCKS):
                    for u in range(UNITS):
                        unpack_unit(t, k, u)
                        if k == BLOCKS - 1 and u >= UNITS - 2 * CHUNKS and u % 2:
                            scale_chunk(t + 1, (u - (UNITS - 2 * CHUNKS)) // 2)
                hi_after = {min(UNITS - 1, ((q + 1) * CJ + PER_UNIT - 1) // PER_UNIT + 1): q for q in range(CHUNKS - 1)}
                done = 0
                for u in range(UNITS):
                    unpack_unit(t + 1, 0, u)
                    if u in hi_after:
                        while done <= hi_after[u]:
                            make_hi(t + 1, done)
                            done += 1
                while done < CHUNKS:
                    make_hi(t + 1, done)
                    done += 1
            for k in range(1, BLOCKS):
                for u in range(UNITS):
                    unpack_unit(T - 1, k, u)

            act.wait_ge(block_summed, BLOCKS * T)
            for b in range(NBANKS):
                take_diagonals(act, nc.scalar.copy, b, (0, 1), diag_act)

            for i, (l, m, mm, n, terms) in enumerate(top_tiles):
                act.wait_ge(top_mm, i + 1)
                dst, bias = activated(l, m, n, (h_top0, h_top1, y), (b_top0c, b_top1c, b_top2c))
                func = ACT.Sigmoid if l == 2 else ACT.Relu
                nc.scalar.activation(dst, mlp_banks[i % 4][0:mm, :], func, bias=bias).then_inc(top_act, 1)

        @block.vector
        def _(dve):
            for i, (src, dst) in enumerate(turns):
                if i % 4 == 0:
                    dve.wait_ge(turned, i // 4 + 1)
                kp, m = src.shape[0], src.shape[1]
                last = nc.vector.tensor_copy(dst, banks[i // 4 % 4][0:m, i % 4 * P:i % 4 * P + kp])
                if i % 4 == 3 or i == len(turns) - 1:
                    last.then_inc(unturned, 1)

            def copy_indices(t, first=False):
                dve.wait_ge(idx_turned, t + 1)
                if not first:
                    dve.wait_ge(idx_ready, 2 * t)
                nc.vector.tensor_copy(idx_t[:, :], idx_ps[0:GK, 0:NI]).then_inc(idx_copied, 1)

            def adopt_indices(t, first=False):
                dve.wait_ge(idx_ready, 2 * t + 2)
                if not first:
                    dve.wait_ge(onehots_ready, UNITS * BLOCKS * t)
                nc.vector.tensor_copy(place[:, :, :], place_next[:, :, :]).then_inc(idx_adopted, 1)
                dve.wait_ge(idx_adopted, t + 1)

            def max_chunk(t, q, first=False):
                if q == 0:
                    dve.wait_ge(table_loaded, 16 * t + 16)
                    if not first:
                        dve.wait_ge(tabmax_ready, t)
                nc.vector.tensor_reduce(rowmax[:, q:q + 1], raw[:, q * CJ:(q + 1) * CJ, :], AX.XY, ALU.max,
                                        apply_absolute_value=True).then_inc(rowmax_part, 1)

            def max_rows(t):
                dve.wait_ge(rowmax_part, CHUNKS * t + CHUNKS)
                nc.vector.tensor_reduce(rowmax[:, CHUNKS:CHUNKS + 1], rowmax[:, 0:CHUNKS], AX.X,
                                        ALU.max).then_inc(rowmax_ready, 1)

            def make_scale(t, first=False):
                dve.wait_ge(tabmax_ready, t + 1)
                if not first:
                    dve.wait_ge(coef_adopted, t)
                    dve.wait_ge(scaled, CHUNKS * t)
                ts = nc.vector.tensor_scalar
                ts(scale_tmp[:, 0:1], rowmax[:, CHUNKS + 1:CHUNKS + 2], TINY, None, ALU.max).then_inc(scale_step, 1)
                dve.wait_ge(scale_step, 2 * t + 1)
                ts(scale_tmp[:, 1:2].bitcast(I32), scale_tmp[:, 0:1].bitcast(I32), EXP_MASK, None,
                   ALU.bitwise_and).then_inc(scale_step, 1)
                dve.wait_ge(scale_step, 2 * t + 2)
                ts(coef_next[:, 0:1], scale_tmp[:, 1:2], COUNT_UNIT * 2.0 ** -HI_EXP, None, ALU.mult)
                ts(coef_next[:, 1:2], scale_tmp[:, 1:2], COUNT_UNIT * 2.0 ** -(HI_EXP + LO_SHIFT), None, ALU.mult)
                ts(coef_next[:, 2:3].bitcast(I32), scale_tmp[:, 1:2].bitcast(I32), -1.0,
                   float((2 * 127 + HI_EXP) * EXP_UNIT), ALU.mult, ALU.add).then_inc(scale_ready, 1)

            def adopt_coef(t, first=False):
                dve.wait_ge(scale_ready, t + 1)
                if not first:
                    dve.wait_ge(pooled_ready, BLOCKS * t)
                nc.vector.tensor_copy(coef[:, :], coef_next[:, 0:2]).then_inc(coef_adopted, 1)
                dve.wait_ge(coef_adopted, t + 1)

            def onehot_unit(t, k, u, first=False):
                n = UNITS * (BLOCKS * t + k) + u
                if not (first and u < 2):
                    dve.wait_ge(unit_counted, n - 1)
                for g in units_of(u):
                    r, i = UG * (u % 2) + g % UG, k * GROUPS + g
                    nc.vector.tensor_scalar(onehot_p[:, r, :], iota_cols[0:GK, 0:P], place[:, 0, i:i + 1], None,
                                            ALU.is_equal)
                    last = nc.vector.tensor_scalar(onehot_c[:, r, :], iota_cols[0:GK, :], place[:, 1, i:i + 1],
                                                   place[:, 2, i:i + 1], ALU.is_equal, ALU.mult)
                last.then_inc(onehots_ready, 1)

            def pool_bags(t, k, first=False):
                n = BLOCKS * t + k
                dve.wait_ge(block_summed, n + 1)
                nc.vector.tensor_scalar(lo_sum[:, :], acc[k % 2][D:2 * D, 0:NB], coef[D:2 * D, 1:2], None,
                                        ALU.mult).then_inc(lo_taken, 1)
                dve.wait_ge(lo_taken, n + 1)
                dve.wait_ge(pooled_free, n + 1)
                nc.vector.scalar_tensor_tensor(pooled[:, k % 2, :], acc[k % 2][0:D, 0:NB], coef[0:D, 0:1],
                                               lo_sum[:, :], ALU.mult, ALU.add).then_inc(pooled_ready, 1)
                dve.wait_ge(pooled_ready, n + 1)
                nc.vector.sem_inc(acc_free, 1)

            dve.wait_ge(consts_ready, 3)
            dve.wait_ge(bot_stored, 16)
            nc.vector.sem_inc(acc_free, 2)
            copy_indices(0, first=True)
            for q in range(CHUNKS):
                max_chunk(0, q, first=True)
            max_rows(0)
            make_scale(0, first=True)
            adopt_coef(0, first=True)
            adopt_indices(0, first=True)
            for u in range(UNITS):
                onehot_unit(0, 0, u, first=True)
            AFTER = 3
            with dve.Fori(0, T - 1) as t:
                for u in range(UNITS):
                    onehot_unit(t, 1, u)
                for u in range(UNITS):
                    onehot_unit(t, 2, u)
                    if u == AFTER:
                        pool_bags(t, 0)
                        copy_indices(t + 1)
                    if AFTER + 2 <= u < AFTER + 2 + CHUNKS:
                        max_chunk(t + 1, u - AFTER - 2)
                    if u == AFTER + 2 + CHUNKS:
                        max_rows(t + 1)
                for u in range(UNITS):
                    onehot_unit(t, 3, u)
                    if u == AFTER:
                        pool_bags(t, 1)
                        make_scale(t + 1)
                adopt_indices(t + 1)
                for u in range(UNITS):
                    onehot_unit(t + 1, 0, u)
                    if u == AFTER:
                        pool_bags(t, 2)
                pool_bags(t, 3)
                adopt_coef(t + 1)
            for k in range(1, BLOCKS):
                for u in range(UNITS):
                    onehot_unit(T - 1, k, u)
                    if u == AFTER and k >= 2:
                        pool_bags(T - 1, k - 2)
            pool_bags(T - 1, BLOCKS - 2)
            pool_bags(T - 1, BLOCKS - 1)

            for b in range(NBANKS):
                take_diagonals(dve, nc.vector.tensor_copy, b, (2, 3), diag_dve)


_INS = ["r_dense_x", "r_indices", "L0_rec_tables"] + [
    f"L0_rec_{x}_{part}{i}" for part in ("bot", "top") for i in range(3) for x in ("w", "b")]


def kernel(**inputs):
    import numpy as _np
    import concourse.bacc as _bacc
    from concourse import mybir as _mybir
    from concourse.bass_utils import run_bass_kernel_spmd as _run

    nc = _bacc.Bacc("TRN2", target_bir_lowering=False, num_devices=1, dynamic_dma_scratch_size=2048)
    arrays, args = {}, {}
    for name in _INS:
        a = _np.ascontiguousarray(inputs[name])
        arrays[f"in_{name}"] = a
        args[name] = nc.dram_tensor(f"in_{name}", a.shape, _mybir.dt.from_np(a.dtype), kind="ExternalInput").ap()
    B = args["r_dense_x"].shape[0]
    out = nc.dram_tensor("out", (B, 1), _mybir.dt.float32, kind="ExternalOutput").ap()

    def layers(x, part):
        return [args[f"L0_rec_{x}_{part}{i}"] for i in range(3)]

    build(nc, args["r_dense_x"], args["r_indices"], args["L0_rec_tables"], layers("w", "bot"), layers("b", "bot"),
          layers("w", "top"), layers("b", "top"), out)
    r = _run(nc, [arrays], core_ids=[0])
    return r.results[0]["out"]
```

```python
from contextlib import ExitStack

import concourse.bass as bass
from concourse import mybir

ALU = mybir.AluOpType
ACT = mybir.ActivationFunctionType
AX = mybir.AxisListType
F32 = mybir.dt.float32
F16 = mybir.dt.float16
BF16 = mybir.dt.bfloat16
I32 = mybir.dt.int32
U32 = mybir.dt.uint32
I16 = mybir.dt.int16
F8 = mybir.dt.float8e3

P = 128
QUAD = 32
BANK = 512

ROUND = 1.5 * 2.0 ** 23
HI_EXP = 14
LO_SHIFT = 11
COUNT_UNIT = 2.0 ** 6
EXP_UNIT = 2 ** 23
EXP_MASK = 0x7F800000
TINY = 2.0 ** -100


def build(nc, dense_x, indices, tables, w_bot, b_bot, w_top, b_top, out):
    T, B, L = indices.shape
    _, ROWS, D = tables.shape
    SLOTS = T + 1
    TG = 5
    TP = T - TG

    SPAN = -(-ROWS // P)
    COLS = -(-SPAN // 3)
    ABSENT = SPAN * P
    GS = P // L
    GK = GS * L
    GC = GS * COLS
    NB = BANK
    BLOCKS = B // NB
    GROUPS = -(-NB // GS)
    TAIL = NB - (GROUPS - 1) * GS
    UG = 4
    UNITS = -(-GROUPS // UG)
    PAIRS = UNITS // 2
    BPAD = GROUPS * GS
    CHUNKS = 7
    CJ = SPAN // CHUNKS
    assert B % NB == 0 and UNITS % 2 == 0 and BLOCKS % 2 == 0 and SPAN % CHUNKS == 0
    assert 2 * GC <= BANK and L < 32 and GROUPS <= P and 2 * D == P and SLOTS <= QUAD
    assert TP * ROWS + ABSENT <= T * ROWS
    assert TG * BLOCKS == TP - 1

    NBOT = [dense_x.shape[1]] + [w.shape[0] for w in w_bot]
    NTOP = [w_top[0].shape[1]] + [w.shape[0] for w in w_top]
    NF = NTOP[0]
    FCH = -(-NF // P)
    CHUNK_B = B // NB
    PAIR_ROW = [D + i * (i - 1) // 2 for i in range(SLOTS)]
    assert NF == PAIR_ROW[-1] + SLOTS - 1 and NTOP[3] == 1 and NBOT[3] == D

    rows_flat = tables.rearrange("t n d -> (t n) d")
    pooled_dram = nc.dram_tensor("pooled", [(TP + 1) * BLOCKS, D, NB], F32, kind="Internal").ap()
    gathered_dram = nc.dram_tensor("gathered", [1 + TG * BLOCKS, D, NB], F32, kind="Internal").ap()

    def units_of(u):
        return range(u * UG, min((u + 1) * UG, GROUPS))

    ctx = ExitStack()
    with ctx:
        def sem(name):
            return ctx.enter_context(nc.semaphore(name))

        weights_in = sem("weights_in")
        consts_ready = sem("consts_ready")
        const_step = sem("const_step")
        turned = sem("turned")
        unturned = sem("unturned")
        bot_mm = sem("bot_mm")
        bot_act = sem("bot_act")
        bot_stored = sem("bot_stored")
        table_loaded = sem("table_loaded")
        idx_loaded = sem("idx_loaded")
        idx_converted = sem("idx_converted")
        idx_turned = sem("idx_turned")
        idx_copied = sem("idx_copied")
        idx_step = sem("idx_step")
        idx_ready = sem("idx_ready")
        idx_adopted = sem("idx_adopted")
        rowmax_part = sem("rowmax_part")
        rowmax_ready = sem("rowmax_ready")
        tabmax_ready = sem("tabmax_ready")
        scale_step = sem("scale_step")
        scale_ready = sem("scale_ready")
        coef_adopted = sem("coef_adopted")
        weighted = sem("weighted")
        scaled = sem("scaled")
        hi_ready = sem("hi_ready")
        diff_ready = sem("diff_ready")
        parts_ready = sem("parts_ready")
        pool_waited = sem("pool_waited")
        chunk_used = sem("chunk_used")
        onehots_ready = sem("onehots_ready")
        unit_counted = sem("unit_counted")
        counts_ready = sem("counts_ready")
        block_summed = sem("block_summed")
        acc_free = sem("acc_free")
        lo_taken = sem("lo_taken")
        pooled_ready = sem("pooled_ready")
        pooled_stored = sem("pooled_stored")
        pooled_free = sem("pooled_free")
        look_loaded = sem("look_loaded")
        look_ready = sem("look_ready")
        look_free = sem("look_free")
        gathered = [sem(f"gathered{c}") for c in range(NB // P)]
        bags_ready = sem("bags_ready")
        bags_turned = sem("bags_turned")
        bags_copied = sem("bags_copied")
        bags_stored = sem("bags_stored")
        bags_free = sem("bags_free")
        slots_in = [sem(f"slots_in{i}") for i in range(2)]
        pads_zeroed = sem("pads_zeroed")
        dense_in = sem("dense_in")
        grams_ready = sem("grams_ready")
        diag_act = sem("diag_act")
        diag_dve = sem("diag_dve")
        top_in = sem("top_in")
        top_turned = sem("top_turned")
        top_unturned = sem("top_unturned")
        pairs_in = [sem(f"pairs_in{k}") for k in range(BLOCKS)]
        top_mm = sem("top_mm")
        top_act = sem("top_act")
        out_stored = sem("out_stored")

        def sb(stack, name, shape, dt):
            return stack.enter_context(nc.sbuf_tensor(name, shape, dt))

        ident = sb(ctx, "ident", [P, P], F32)
        iota_by_unit = sb(ctx, "iota_by_unit", [P, P, UG], BF16)
        sample_mask = sb(ctx, "sample_mask", [P, GS, UG], BF16)
        sample_base = sb(ctx, "sample_base", [P, 1], F32)
        w_top2T = sb(ctx, "w_top2T", [P, NTOP[2] // P], F32)
        b_top0c = sb(ctx, "b_top0c", [P, NTOP[1] // P], F32)
        b_top1c = sb(ctx, "b_top1c", [P, NTOP[2] // P], F32)
        b_top2c = sb(ctx, "b_top2c", [1, 1], F32)
        idx_raw = sb(ctx, "idx_raw", [GROUPS, BLOCKS, GK], I32)

        early = ExitStack()
        w_bot0r = sb(early, "w_bot0r", [P, NBOT[1] // P, NBOT[0]], F32)
        w_bot1r = sb(early, "w_bot1r", [P, NBOT[2] // P, NBOT[1]], F32)
        w_bot2r = sb(early, "w_bot2r", [D, NBOT[2]], F32)
        xr = sb(early, "xr", [P, B // P, NBOT[0]], F32)
        xT = sb(early, "xT", [NBOT[0], B], F32)
        w_bot0T = sb(early, "w_bot0T", [NBOT[0], NBOT[1]], F32)
        w_bot1T = sb(early, "w_bot1T", [P, NBOT[1] // P, NBOT[2]], F32)
        w_bot2T = sb(early, "w_bot2T", [P, NBOT[2] // P, D], F32)
        b_bot0c = sb(early, "b_bot0c", [P, NBOT[1] // P], F32)
        b_bot1c = sb(early, "b_bot1c", [P, NBOT[2] // P], F32)
        b_bot2c = sb(early, "b_bot2c", [D, 1], F32)
        h_bot0 = sb(early, "h_bot0", [P, NBOT[1] // P, B], F32)
        h_bot1 = sb(early, "h_bot1", [P, NBOT[2] // P, B], F32)
        x_bot = sb(early, "x_bot", [D, B], F32)
        iota_p = sb(early, "iota_p", [P, 1], F32)
        iota_s = sb(early, "iota_s", [P, GS, UG], BF16)
        early.close()

        loop = ExitStack()
        counts = [sb(loop, f"counts{i}", [P, COLS, BPAD], I32) for i in range(2)]
        count_bytes = [c[:, :, :].rearrange("p c b -> p (c b)").bitcast(F8).rearrange(
            "p (c b f) -> p c b f", b=BPAD, f=4) for c in counts]
        raw = sb(loop, "raw", [P, SPAN, D], F32)
        parts = sb(loop, "parts", [P, SPAN, 2 * D], F16)
        onehot_p = sb(loop, "onehot_p", [GK, 2, 2, P, UG], BF16)
        onehot_c = sb(loop, "onehot_c", [GK, 2, 2, COLS, GS, UG], BF16)
        weighted_c = sb(loop, "weighted_c", [GK, UNITS, COLS, UG], BF16)
        idx_f = sb(loop, "idx_f", [GROUPS, BLOCKS, GK], F32)
        NI = BLOCKS * GROUPS
        idx_t = sb(loop, "idx_t", [GK, NI], F32)
        scratch = sb(loop, "scratch", [GK, NI], F32)
        NIP = NI + UNITS * UG - GROUPS
        place_next = sb(loop, "place_next", [GK, 3, NIP], BF16)
        place = sb(loop, "place", [GK, 3, NIP], BF16)
        look = sb(loop, "look", [P, NB // P, L], I32)
        look_in = sb(loop, "look_in", [P, NB // P, L], I32)
        row_base = sb(loop, "row_base", [P, TG * BLOCKS], I32)
        bags = sb(loop, "bags", [P, NB // P, D], F32)
        bags_out = sb(loop, "bags_out", [P, NB // P, D], F32)
        bags_t = sb(loop, "bags_t", [P, NB // 2], F32)
        rowmax = sb(loop, "rowmax", [P, CHUNKS + 2], F32)
        scale_tmp = sb(loop, "scale_tmp", [P, 4], F32)
        coef_next = sb(loop, "coef_next", [P, 3], F32)
        coef = sb(loop, "coef", [P, 2], F32)
        lo_sum = sb(loop, "lo_sum", [D, NB], F32)
        pooled = sb(loop, "pooled_sb", [D, 2, NB], F32)
        loop.close()

        late = ExitStack()
        HG = 64
        TILES = NB // (2 * HG)
        slots = [sb(late, f"slots{i}", [P, CHUNK_B, QUAD, HG], F32) for i in range(2)]
        zt = sb(late, "zt", [P, SLOTS, NB], F32)
        feats = sb(late, "feats", [P, FCH, B], F32)
        w_top0r = sb(late, "w_top0r", [P, NTOP[1] // P, NF], F32)
        w_top1r = sb(late, "w_top1r", [P, NTOP[2] // P, NTOP[1]], F32)
        w_top0T = sb(late, "w_top0T", [P, FCH, NTOP[1]], F32)
        w_top1T = sb(late, "w_top1T", [P, NTOP[1] // P, NTOP[2]], F32)
        late.close()
        final = ExitStack()
        h_top0 = sb(final, "h_top0", [P, NTOP[1] // P, B], F32)
        h_top1 = sb(final, "h_top1", [P, NTOP[2] // P, B], F32)
        y = sb(final, "y", [1, B], F32)
        final.close()

        ps = ctx.enter_context(nc.psum_tensor("ps", [P, 8, BANK], F32))
        banks = [ps[:, i, :] for i in range(8)]
        unit_ps = [ps[:, 2 * i:2 * i + 2, :].rearrange("p b (h c) -> p (b h) c", h=2) for i in range(2)]
        acc = banks[4:6]
        idx_ps, bags_ps = banks[6], banks[7]
        bot_banks = [banks[4], banks[5], banks[7]]
        top_banks = banks[4:8]

        block = ctx.enter_context(nc.Block())

        turns = []
        for m in range(B // P):
            turns.append((xr[:, m, :], xT[:, m * P:(m + 1) * P]))
        for m in range(NBOT[1] // P):
            turns.append((w_bot0r[:, m, :], w_bot0T[:, m * P:(m + 1) * P]))
        for m in range(NBOT[2] // P):
            for k in range(NBOT[1] // P):
                turns.append((w_bot1r[:, m, k * P:(k + 1) * P], w_bot1T[:, k, m * P:(m + 1) * P]))
        for k in range(NBOT[2] // P):
            turns.append((w_bot2r[:, k * P:(k + 1) * P], w_bot2T[:, k, :]))
        top_turns = []
        for m in range(NTOP[1] // P):
            for k in range(FCH):
                n = min(P, NF - k * P)
                top_turns.append((w_top0r[:, m, k * P:k * P + n], w_top0T[0:n, k, m * P:(m + 1) * P]))
        for m in range(NTOP[2] // P):
            for k in range(NTOP[1] // P):
                top_turns.append((w_top1r[:, m, k * P:(k + 1) * P], w_top1T[:, k, m * P:(m + 1) * P]))

        weight_loads = [
            (xr[:, :, :], dense_x.rearrange("(m p) k -> p m k", p=P)),
            (w_bot0r[:, :, :], w_bot[0].rearrange("(m p) k -> p m k", p=P)),
            (w_bot1r[:, :, :], w_bot[1].rearrange("(m p) k -> p m k", p=P)),
            (w_bot2r[:, :], w_bot[2]),
            (w_top2T[:, :], w_top[2].rearrange("a (m p) -> p (a m)", p=P)),
            (b_bot0c[:, :], b_bot[0].rearrange("(m p) -> p m", p=P)),
            (b_bot1c[:, :], b_bot[1].rearrange("(m p) -> p m", p=P)),
            (b_bot2c[:, :], b_bot[2].rearrange("(m p) -> p m", p=D)),
            (b_top0c[:, :], b_top[0].rearrange("(m p) -> p m", p=P)),
            (b_top1c[:, :], b_top[1].rearrange("(m p) -> p m", p=P)),
            (b_top2c[:, :], b_top[2].rearrange("(m p) -> p m", p=1)),
        ]

        def layer(K, M, wT, src):
            for n in range(B // NB):
                for m in range(-(-M // P)):
                    mm = min(P, M - m * P)
                    terms = []
                    for k in range(-(-K // P)):
                        kk = min(P, K - k * P)
                        terms.append((wT(k, kk, m, mm), src(k, kk, n)))
                    yield m, mm, n, terms

        bot_layers = [
            list(layer(NBOT[0], NBOT[1], lambda k, kk, m, mm: w_bot0T[:, m * P:m * P + mm],
                       lambda k, kk, n: xT[:, n * NB:(n + 1) * NB])),
            list(layer(NBOT[1], NBOT[2], lambda k, kk, m, mm: w_bot1T[:, k, m * P:m * P + mm],
                       lambda k, kk, n: h_bot0[:, k, n * NB:(n + 1) * NB])),
            list(layer(NBOT[2], NBOT[3], lambda k, kk, m, mm: w_bot2T[:, k, :],
                       lambda k, kk, n: h_bot1[:, k, n * NB:(n + 1) * NB])),
        ]
        top_layers = [
            list(layer(NF, NTOP[1], lambda k, kk, m, mm: w_top0T[0:kk, k, m * P:m * P + mm],
                       lambda k, kk, n: feats[0:kk, k, n * NB:(n + 1) * NB])),
            list(layer(NTOP[1], NTOP[2], lambda k, kk, m, mm: w_top1T[:, k, m * P:m * P + mm],
                       lambda k, kk, n: h_top0[:, k, n * NB:(n + 1) * NB])),
            list(layer(NTOP[2], 1, lambda k, kk, m, mm: w_top2T[:, k:k + 1],
                       lambda k, kk, n: h_top1[:, k, n * NB:(n + 1) * NB])),
        ]
        bot_tiles = [(l, *t) for l, tiles in enumerate(bot_layers) for t in tiles]
        top_tiles = sorted(((l, *t) for l, tiles in enumerate(top_layers) for t in tiles),
                           key=lambda t: (t[0] + t[3], t[0]))

        def needed(tiles, i):
            l, n = tiles[i][0], tiles[i][3]
            done = [j for j, t in enumerate(tiles) if t[0] == l - 1 and t[3] == n]
            return done[-1] + 1 if done else 0

        def pieces(i):
            at, j = PAIR_ROW[i], 0
            while j < i:
                n = min(i - j, P - (at + j) % P)
                yield j, n, (at + j) // P, (at + j) % P
                j += n

        NPIECE = sum(1 for i in range(1, SLOTS) for _ in pieces(i))
        GRAMS = 8
        NGRAM = NB // GRAMS
        GRAMS_PER_TILE = NGRAM // TILES

        PER_UNIT = 4

        def take_diagonals(eng, copy, b, quarters, done):
            r, half, w = b // GRAMS_PER_TILE, b % 2, b % GRAMS_PER_TILE // 2
            g0 = r * 2 * HG + half * HG + GRAMS * w
            eng.wait_ge(grams_ready, b + 1)
            src = ps[:, 2 * (b % 4):2 * (b % 4) + 2, :].rearrange("p a (x k s) -> p (a x) k s", k=CHUNK_B, s=QUAD)
            for k in quarters:
                rows = slice(QUAD * k, QUAD * (k + 1))
                last = copy(zt[rows, :, g0:g0 + GRAMS].rearrange("p s x -> p x s"), src[rows, :, k, 0:SLOTS])
            last.then_inc(done, 1)

        HALVES = 2
        HW = NB // HALVES

        def move_pairs(eng, h, quarters):
            eng.wait_ge(diag_act, NGRAM // HALVES * (h + 1))
            eng.wait_ge(diag_dve, NGRAM // HALVES * (h + 1))
            for k in quarters:
                for i in range(1, SLOTS):
                    for j, n, ch, p0 in pieces(i):
                        eng.dma_start(feats[p0:p0 + n, ch, k * NB + h * HW:k * NB + (h + 1) * HW],
                                      zt[QUAD * k + j:QUAD * k + j + n, i, h * HW:(h + 1) * HW]
                                      ).then_inc(pairs_in[k], 16)

        def turn(pe, items, full, out):
            for i, (src, dst) in enumerate(items):
                if i >= 4 * 4 and i % 4 == 0:
                    pe.wait_ge(out, i // 4 - 3)
                kp, m = src.shape[0], src.shape[1]
                last = nc.tensor.transpose(banks[i // 4 % 4][0:m, i % 4 * P:i % 4 * P + kp], src,
                                           ident[0:kp, 0:kp])
                if i % 4 == 3 or i == len(items) - 1:
                    last.then_inc(full, 1)
            pe.wait_ge(out, -(-len(items) // 4))

        def unturn(dve, items, full, out):
            for i, (src, dst) in enumerate(items):
                if i % 4 == 0:
                    dve.wait_ge(full, i // 4 + 1)
                kp, m = src.shape[0], src.shape[1]
                last = nc.vector.tensor_copy(dst, banks[i // 4 % 4][0:m, i % 4 * P:i % 4 * P + kp])
                if i % 4 == 3 or i == len(items) - 1:
                    last.then_inc(out, 1)

        @block.sync
        def _(sp):
            def load_table(src):
                sp.dma_start(raw[:, :, :], src.rearrange("(p j) d -> p j d", p=P)).then_inc(table_loaded, 16)

            def load_indices(t):
                flat = indices[t].rearrange("b l -> (b l)").rearrange("(k r) -> k r", k=BLOCKS)
                cut = (GROUPS - 1) * GK
                sp.dma_start(idx_raw[0:GROUPS - 1, :, :],
                             flat[:, 0:cut].rearrange("k (g r) -> g k r", r=GK)).then_inc(idx_loaded, 16)
                sp.dma_start(idx_raw[GROUPS - 1:GROUPS, :, 0:TAIL * L],
                             flat[:, cut:NB * L].rearrange("k (g r) -> g k r", g=1)).then_inc(idx_loaded, 16)

            def load_lookups(n):
                flat = indices.rearrange("t b l -> (t b) l")
                sp.dma_start(look_in[:, :, :], flat[bass.ds(n * NB + TP * B, NB), :].rearrange(
                    "(c p) l -> p c l", p=P)).then_inc(look_loaded, 16)

            def store_pooled(t, k):
                sp.wait_ge(pooled_ready, BLOCKS * t + k + 1)
                sp.dma_start(pooled_dram[BLOCKS * t + BLOCKS + k], pooled[:, k % 2, :]).then_inc(pooled_stored, 16)
                sp.wait_ge(pooled_stored, 16 * (BLOCKS * t + k + 1))
                sp.sem_inc(pooled_free, 1)

            def store_bags(n):
                sp.wait_ge(bags_copied, n + 1)
                for h in range(2):
                    dst = gathered_dram[n].rearrange("d (q c b) -> c d q b", c=2, b=P)[h]
                    sp.dma_start(dst, bags_t[h * D:(h + 1) * D, :].rearrange("d (q b) -> d q b", b=P)
                                 ).then_inc(bags_stored, 16)
                sp.wait_ge(bags_stored, 32 * n + 32)
                sp.sem_inc(bags_free, 1)

            sp.sem_inc(bags_free, 1)
            sp.sem_inc(pooled_free, 2)
            sp.wait_ge(const_step, 3)
            load_indices(0)
            load_table(rows_flat[0:SPAN * P, :])
            for dst, src in weight_loads:
                with nc.allow_non_contiguous_dma(reason="small weights and biases"):
                    sp.dma_start(dst, src).then_inc(weights_in, 16)
            with sp.Fori(0, TP - 1) as t:
                sp.wait_ge(look_free, t + 1)
                load_lookups(t)
                sp.wait_ge(idx_converted, t + 1)
                load_indices(t + 1)
                sp.wait_ge(parts_ready, CHUNKS * t + CHUNKS)
                load_table(rows_flat[bass.ds((t + 1) * ROWS, SPAN * P), :])
                store_pooled(t, 0)
                store_pooled(t, 1)
                store_bags(t)
                store_pooled(t, 2)
                store_pooled(t, 3)
            for k in range(BLOCKS):
                store_pooled(TP - 1, k)
            store_bags(TP - 1)
            sp.wait_ge(bags_stored, 32 * TP)

            def load_slots(r):
                if r >= 2:
                    sp.wait_ge(grams_ready, GRAMS_PER_TILE * (r - 1))
                for half in range(2):
                    g0 = r * 2 * HG + half * HG
                    for k in range(CHUNK_B):
                        dst = slots[r % 2][half * D:(half + 1) * D, k, :, :]
                        for src, s0, s1 in ((pooled_dram, 0, TP + 1), (gathered_dram[1:, :, :], TP + 1, SLOTS)):
                            sp.dma_start(dst[:, s0:s1, :], src.rearrange("(s k) d g -> k d s g", k=BLOCKS)[
                                k, :, :, g0:g0 + HG]).then_inc(slots_in[r % 2], 16)

            load_slots(0)
            sp.dma_start(w_top0r[:, :, :], w_top[0].rearrange("(m p) k -> p m k", p=P)).then_inc(top_in, 16)
            sp.dma_start(w_top1r[:, :, :], w_top[1].rearrange("(m p) k -> p m k", p=P)).then_inc(top_in, 16)
            load_slots(1)
            sp.dma_start(feats[0:D, 0, :].rearrange("d (k g) -> d k g", k=BLOCKS),
                         pooled_dram[0:BLOCKS, :, :].rearrange("k d g -> d k g")).then_inc(dense_in, 16)
            load_slots(2)
            load_slots(3)
            assert TILES == 4
            move_pairs(sp, 0, range(CHUNK_B))
            move_pairs(sp, 1, range(0, 2))
            sp.wait_ge(top_act, len(top_tiles))
            sp.dma_start(out.rearrange("b a -> a b"), y[:, :]).then_inc(out_stored, 16)
            sp.wait_ge(out_stored, 16)

        @block.gpsimd
        def _(pool):
            def await_alone(semaphore, value):
                pool.wait_ge(semaphore, value)
                pool.sem_inc(pool_waited, 1)

            nc.gpsimd.memset(ident[:, :], 0.0).then_inc(const_step, 1)
            nc.gpsimd.iota(iota_p[:, :], pattern=[[0, 1]], base=0, channel_multiplier=1,
                           allow_small_or_imprecise_dtypes=True).then_inc(const_step, 1)
            nc.gpsimd.memset(idx_raw[:, :, :], ABSENT).then_inc(const_step, 1)
            pool.wait_ge(const_step, 3)
            nc.gpsimd.affine_select(out=ident[:, :], in_=ident[:, :], compare_op=ALU.not_equal, fill=1.0,
                                    base=0, pattern=[[-1, P]], channel_multiplier=1).then_inc(consts_ready, 1)
            nc.gpsimd.iota(iota_by_unit[:, :, :], pattern=[[1, P], [0, UG]], base=0, channel_multiplier=0,
                           allow_small_or_imprecise_dtypes=True).then_inc(const_step, 1)
            nc.gpsimd.iota(iota_s[:, :, :], pattern=[[1, GS], [0, UG]], base=0, channel_multiplier=0,
                           allow_small_or_imprecise_dtypes=True).then_inc(const_step, 1)
            nc.gpsimd.iota(row_base[:, :], pattern=[[ROWS, TG], [0, BLOCKS]], base=TP * ROWS,
                           channel_multiplier=0).then_inc(const_step, 1)
            nc.gpsimd.memset(bags_out[:, :, :], 0.0).then_inc(bags_ready, 1)
            nc.gpsimd.memset(place_next[:, :, :], 0.0).then_inc(const_step, 1)
            nc.gpsimd.tensor_scalar(iota_p[:, :], iota_p[:, :], -(L - 1) / 2, 1.0 / L,
                                    ALU.add, ALU.mult).then_inc(const_step, 1)
            pool.wait_ge(const_step, 8)
            nc.gpsimd.tensor_scalar(sample_base[:, :], iota_p[:, :], ROUND, -ROUND,
                                    ALU.add, ALU.add).then_inc(const_step, 1)
            pool.wait_ge(const_step, 9)
            nc.gpsimd.tensor_scalar(sample_mask[:, :, :], iota_s[:, :, :], sample_base[:, :], None,
                                    ALU.is_equal).then_inc(consts_ready, 1)

            STEPS = 8
            part_i, col_i, weight_i = (place_next[:, i, 0:NI] for i in range(3))

            def convert_indices(t):
                await_alone(idx_loaded, 32 * t + 32)
                nc.gpsimd.tensor_copy(idx_f[:, :, :], idx_raw[:, :, :]).then_inc(idx_converted, 1)

            def place_indices(t, first=False):
                n = [0]

                def step(ins):
                    n[0] += 1
                    ins.then_inc(idx_step, 1)
                    await_alone(idx_step, STEPS * t + n[0])

                pool.wait_ge(idx_copied, t + 1)
                if not first:
                    pool.wait_ge(idx_adopted, t)
                pool.sem_inc(pool_waited, 1)
                ts, tt = nc.gpsimd.tensor_scalar, nc.gpsimd.tensor_tensor
                step(ts(scratch[:, :], idx_t[:, :], -(SPAN - 1) / 2, 1.0 / SPAN, ALU.add, ALU.mult))
                step(ts(part_i, scratch[:, :], ROUND, -ROUND, ALU.add, ALU.add))
                step(ts(scratch[:, :], part_i, -float(SPAN), 0.0, ALU.mult, ALU.add))
                step(tt(idx_t[:, :], idx_t[:, :], scratch[:, :], ALU.add))
                step(ts(scratch[:, :], idx_t[:, :], -(COLS - 1) / 2, 1.0 / COLS, ALU.add, ALU.mult))
                step(ts(scratch[:, :], scratch[:, :], ROUND, -ROUND, ALU.add, ALU.add))
                step(ts(weight_i.bitcast(I16), scratch[:, :], 8.0 * 128, 127.0 * 128, ALU.mult, ALU.add))
                step(ts(scratch[:, :], scratch[:, :], -float(COLS), 0.0, ALU.mult, ALU.add))
                assert n[0] == STEPS
                tt(col_i, idx_t[:, :], scratch[:, :], ALU.add).then_inc(idx_ready, 1)

            def table_max(t):
                await_alone(rowmax_ready, t + 1)
                nc.gpsimd.partition_all_reduce(rowmax[:, CHUNKS + 1:CHUNKS + 2], rowmax[:, CHUNKS:CHUNKS + 1], P,
                                               bass.bass_isa.ReduceOp.max).then_inc(tabmax_ready, 1)

            def make_lo(t, q):
                c = slice(q * CJ, (q + 1) * CJ)
                pool.wait_ge(hi_ready, CHUNKS * t + q + 1)
                nc.gpsimd.tensor_tensor(raw[:, c, :], raw[:, c, :], parts[:, c, 0:D],
                                        ALU.subtract).then_inc(diff_ready, 1)
                await_alone(diff_ready, CHUNKS * t + q + 1)
                nc.gpsimd.tensor_scalar(parts[:, c, D:2 * D], raw[:, c, :], 2.0 ** LO_SHIFT, 0.0, ALU.mult,
                                        ALU.add).then_inc(parts_ready, 1)

            def make_lookups(n):
                await_alone(look_loaded, 16 * n + 16)
                nc.gpsimd.tensor_tensor(look[:, :, :], look_in[:, :, :],
                                        row_base[:, n:n + 1].to_broadcast([P, NB // P, L]) if isinstance(n, int)
                                        else row_base[:, bass.ds(n, 1)].to_broadcast([P, NB // P, L]),
                                        ALU.add).then_inc(look_ready, 1)
                await_alone(look_ready, n + 1)
                pool.sem_inc(look_free, 1)

            def gather(n, i):
                l, c = divmod(i, NB // P)
                if l:
                    await_alone(gathered[c], 16 * (L * n + l))
                nc.gpsimd.indirect_dma_start(
                    bags[:, c, :], None, rows_flat,
                    bass.IndirectOffsetOnAxis(ap=look[:, c, l:l + 1].bitcast(U32), axis=0),
                    compute_op=ALU.add if l else ALU.bypass).then_inc(gathered[c], 16)

            def end_gathers(n):
                for c in range(NB // P):
                    pool.wait_ge(gathered[c], 16 * (L * n + L))
                await_alone(bags_turned, n + 1)
                nc.gpsimd.tensor_copy(bags_out[:, :, :], bags[:, :, :]).then_inc(bags_ready, 1)
                await_alone(bags_ready, n + 2)

            convert_indices(0)
            place_indices(0, first=True)
            table_max(0)
            for q in range(CHUNKS):
                make_lo(0, q)
            pool.sem_inc(look_free, 1)
            G = NB // P * L
            cuts = [G * 30 // 100, G * 45 // 100, G * 70 // 100]
            with pool.Fori(0, TP - 1) as t:
                convert_indices(t + 1)
                make_lookups(t)
                for i in range(0, cuts[0]):
                    gather(t, i)
                place_indices(t + 1)
                for i in range(cuts[0], cuts[1]):
                    gather(t, i)
                table_max(t + 1)
                for i in range(cuts[1], cuts[2]):
                    gather(t, i)
                at = cuts[2]
                for q in range(CHUNKS):
                    make_lo(t + 1, q)
                    until = cuts[2] + (G - cuts[2]) * (q + 1) // CHUNKS
                    for i in range(at, until):
                        gather(t, i)
                    at = until
                end_gathers(t)
            pool.wait_ge(block_summed, BLOCKS * TP)
            for q in range(2):
                nc.gpsimd.memset(slots[q][:, :, SLOTS:QUAD, :], 0.0).then_inc(pads_zeroed, 1)

        @block.tensor
        def _(pe):
            def mlp(tiles, into, mm_sem, act_sem, inputs=lambda n: None):
                for i, (l, m, mm, n, terms) in enumerate(tiles):
                    if l == 0 and m == 0:
                        inputs(n)
                    ready = max(needed(tiles, i), i + 1 - len(into))
                    if ready > 0:
                        pe.wait_ge(act_sem, ready)
                    for k, (w, x) in enumerate(terms):
                        last = nc.tensor.matmul(into[i % len(into)][0:mm, :], w, x, start=(k == 0),
                                                stop=(k == len(terms) - 1))
                    last.then_inc(mm_sem, 1)

            def turn_indices(t, first=False):
                pe.wait_ge(idx_converted, t + 1)
                if not first:
                    pe.wait_ge(idx_copied, t)
                for k in range(BLOCKS):
                    last = nc.tensor.transpose(idx_ps[0:GK, k * GROUPS:(k + 1) * GROUPS], idx_f[:, k, :],
                                               ident[0:GROUPS, 0:GROUPS])
                last.then_inc(idx_turned, 1)

            def turn_bags(n):
                pe.wait_ge(bags_ready, n + 1)
                for q in range(NB // P // 2):
                    last = nc.tensor.transpose(bags_ps[:, q * P:(q + 1) * P],
                                               bags_out[:, 2 * q:2 * q + 2, :].rearrange("p c d -> p (c d)"),
                                               ident[:, :])
                last.then_inc(bags_turned, 1)

            def count_unit(t, k, u, first=False):
                n = UNITS * (BLOCKS * t + k) + u
                if u % 2 == 0:
                    pe.wait_ge(onehots_ready, PAIRS * (BLOCKS * t + k) + u // 2 + 1)
                if not (first and u < 2):
                    pe.wait_ge(counts_ready, n - 1)
                r = (PAIRS * k + u // 2) % 2
                for g in units_of(u):
                    x = g % UG
                    last = nc.tensor.matmul(unit_ps[u % 2][:, x, 0:GC], onehot_p[:, r, u % 2, :, x],
                                            onehot_c[:, r, u % 2, :, :, x].rearrange("p c s -> p (c s)"),
                                            start=True, stop=True)
                last.then_inc(unit_counted, 1)

            def await_rows(t, k, j0, j1):
                n = BLOCKS * t + k
                if j0 == 0:
                    pe.wait_ge(counts_ready, UNITS * n + UNITS)
                    pe.wait_ge(acc_free, n + 1)
                for j in range(j0, j1):
                    if k == 0 and j % CJ == 0:
                        pe.wait_ge(parts_ready, CHUNKS * t + j // CJ + 1)

            def sum_rows(t, k, j):
                mm = nc.tensor.matmul(acc[k % 2][:, 0:NB], parts[:, j, :],
                                      count_bytes[k % 2][:, j % COLS, 0:NB, j // COLS],
                                      start=(j == 0), stop=(j == SPAN - 1))
                if j == SPAN - 1:
                    mm.then_inc(block_summed, 1)
                elif k == BLOCKS - 1 and j % CJ == CJ - 1:
                    mm.then_inc(chunk_used, 1)

            def phase(t, k, tn, kn):
                for u in range(UNITS):
                    j1 = SPAN if u == UNITS - 1 else PER_UNIT * (u + 1)
                    await_rows(t, k, PER_UNIT * u, j1)
                    count_unit(tn, kn, u)
                    for j in range(PER_UNIT * u, PER_UNIT * (u + 1)):
                        sum_rows(t, k, j)
                for j in range(PER_UNIT * UNITS, SPAN):
                    sum_rows(t, k, j)

            pe.wait_ge(consts_ready, 1)
            turn_indices(0, first=True)
            pe.wait_ge(weights_in, 16 * len(weight_loads))
            turn(pe, turns, turned, unturned)
            mlp(bot_tiles, bot_banks, bot_mm, bot_act)
            pe.wait_ge(bot_act, len(bot_tiles))
            for u in range(UNITS):
                count_unit(0, 0, u, first=True)

            with pe.Fori(0, TP - 1) as t:
                phase(t, 0, t, 1)
                turn_indices(t + 1)
                phase(t, 1, t, 2)
                turn_bags(t)
                phase(t, 2, t, 3)
                phase(t, 3, t + 1, 0)
            for k in range(BLOCKS - 1):
                phase(TP - 1, k, TP - 1, k + 1)
            turn_bags(TP - 1)
            await_rows(TP - 1, BLOCKS - 1, 0, SPAN)
            for j in range(SPAN):
                sum_rows(TP - 1, BLOCKS - 1, j)

            pe.wait_ge(acc_free, BLOCKS * TP + 2)
            pe.wait_ge(counts_ready, UNITS * BLOCKS * TP)
            pe.wait_ge(top_in, 32)
            turn(pe, top_turns, top_turned, top_unturned)
            pe.wait_ge(bags_copied, TP)
            pe.wait_ge(pads_zeroed, 2)
            for b in range(NGRAM):
                r, half, w = b // GRAMS_PER_TILE, b % 2, b % GRAMS_PER_TILE // 2
                if b % GRAMS_PER_TILE == 0:
                    pe.wait_ge(slots_in[r % 2], 16 * 4 * CHUNK_B * (r // 2 + 1))
                if b >= 4:
                    pe.wait_ge(diag_act, b - 3)
                    pe.wait_ge(diag_dve, b - 3)
                tile = slots[r % 2][half * D:(half + 1) * D, :, :, :].rearrange("p k s g -> p g (k s)")
                for x in range(GRAMS):
                    g = GRAMS * w + x
                    last = nc.tensor.matmul(banks[2 * (b % 4) + x // 4][:, x % 4 * P:(x % 4 + 1) * P], tile[:, g, :],
                                            tile[:, g, :], start=True, stop=True)
                last.then_inc(grams_ready, 1)

            pe.wait_ge(diag_act, NGRAM)
            pe.wait_ge(diag_dve, NGRAM)
            pe.wait_ge(dense_in, 16)
            mlp(top_tiles, top_banks, top_mm, top_act,
                inputs=lambda n: pe.wait_ge(pairs_in[n], 16 * NPIECE * HALVES))

        @block.scalar
        def _(act):
            def activated(l, m, n, outs, biases):
                cols = slice(n * NB, (n + 1) * NB)
                return (outs[l][:, m, cols] if l < 2 else outs[l][:, cols]), biases[l][:, m:m + 1]

            def scale_chunk(t, q):
                c = slice(q * CJ, (q + 1) * CJ)
                if q == 0:
                    act.wait_ge(scale_ready, t + 1)
                nc.scalar.activation(raw[:, c, :], raw[:, c, :], ACT.Copy,
                                     scale=coef_next[:, 2:3]).then_inc(scaled, 1)

            def make_hi(t, q, first=False):
                c = slice(q * CJ, (q + 1) * CJ)
                act.wait_ge(scaled, CHUNKS * t + q + 1)
                if not first:
                    if q == CHUNKS - 1:
                        act.wait_ge(block_summed, BLOCKS * t)
                    else:
                        act.wait_ge(chunk_used, (CHUNKS - 1) * (t - 1) + q + 1)
                nc.scalar.copy(parts[:, c, 0:D], raw[:, c, :]).then_inc(hi_ready, 1)

            def copy_bags(n):
                act.wait_ge(bags_turned, n + 1)
                act.wait_ge(bags_free, n + 1)
                nc.scalar.copy(bags_t[:, :], bags_ps[:, 0:NB // 2]).then_inc(bags_copied, 1)

            def unpack_unit(t, k, u, first=False):
                n = UNITS * (BLOCKS * t + k) + u
                act.wait_ge(unit_counted, n + 1)
                g = len(units_of(u))
                nc.scalar.copy(
                    counts[k % 2][:, :, u * UG * GS:(u * UG + g) * GS].rearrange("p c (g s) -> p g c s", s=GS),
                    unit_ps[u % 2][:, 0:g, 0:GC].rearrange("p g (c s) -> p g c s", s=GS),
                ).then_inc(counts_ready, 1)

            for i, (l, m, mm, n, terms) in enumerate(bot_tiles):
                act.wait_ge(bot_mm, i + 1)
                dst, bias = activated(l, m, n, (h_bot0, h_bot1, x_bot), (b_bot0c, b_bot1c, b_bot2c))
                nc.scalar.activation(dst, bot_banks[i % 3][0:mm, :], ACT.Relu, bias=bias).then_inc(bot_act, 1)
                if l == 1:
                    if m == 0 and n == 0:
                        for q in range(CHUNKS):
                            scale_chunk(0, q)
                    elif m == 0 and n == 1:
                        for q in range(CHUNKS):
                            make_hi(0, q, first=True)
            act.wait_ge(bot_act, len(bot_tiles))
            act.dma_start(pooled_dram[0:BLOCKS, :, :].rearrange("k d g -> d k g"),
                          x_bot[:, :].rearrange("d (k g) -> d k g", k=BLOCKS)).then_inc(bot_stored, 16)
            act.wait_ge(bot_stored, 16)
            for u in range(UNITS):
                unpack_unit(0, 0, u, first=True)
            with act.Fori(0, TP - 1) as t:
                for k in range(1, BLOCKS):
                    for u in range(UNITS):
                        unpack_unit(t, k, u)
                        if k == BLOCKS - 1 and u == 3:
                            copy_bags(t)
                        if k == BLOCKS - 1 and u >= UNITS - 2 * CHUNKS and u % 2:
                            scale_chunk(t + 1, (u - (UNITS - 2 * CHUNKS)) // 2)
                hi_after = {min(UNITS - 1, ((q + 1) * CJ + PER_UNIT - 1) // PER_UNIT + 1): q for q in range(CHUNKS - 1)}
                done = 0
                for u in range(UNITS):
                    unpack_unit(t + 1, 0, u)
                    if u in hi_after:
                        while done <= hi_after[u]:
                            make_hi(t + 1, done)
                            done += 1
                while done < CHUNKS:
                    make_hi(t + 1, done)
                    done += 1
            for k in range(1, BLOCKS):
                for u in range(UNITS):
                    unpack_unit(TP - 1, k, u)
            copy_bags(TP - 1)

            act.wait_ge(block_summed, BLOCKS * TP)
            for b in range(NGRAM):
                take_diagonals(act, nc.scalar.copy, b, (0, 1), diag_act)
            move_pairs(act, 1, range(2, CHUNK_B))

            for i, (l, m, mm, n, terms) in enumerate(top_tiles):
                act.wait_ge(top_mm, i + 1)
                dst, bias = activated(l, m, n, (h_top0, h_top1, y), (b_top0c, b_top1c, b_top2c))
                func = ACT.Sigmoid if l == 2 else ACT.Relu
                nc.scalar.activation(dst, top_banks[i % 4][0:mm, :], func, bias=bias).then_inc(top_act, 1)

        @block.vector
        def _(dve):
            def copy_indices(t, first=False):
                dve.wait_ge(idx_turned, t + 1)
                if not first:
                    dve.wait_ge(idx_ready, t)
                nc.vector.tensor_copy(idx_t[:, :], idx_ps[0:GK, 0:NI]).then_inc(idx_copied, 1)

            def adopt_indices(t, first=False):
                dve.wait_ge(idx_ready, t + 1)
                if not first:
                    dve.wait_ge(onehots_ready, PAIRS * BLOCKS * t)
                nc.vector.tensor_copy(place[:, :, :], place_next[:, :, :]).then_inc(idx_adopted, 1)
                dve.wait_ge(idx_adopted, t + 1)

            def max_chunk(t, q, first=False):
                if q == 0:
                    dve.wait_ge(table_loaded, 16 * t + 16)
                    if not first:
                        dve.wait_ge(tabmax_ready, t)
                nc.vector.tensor_reduce(rowmax[:, q:q + 1], raw[:, q * CJ:(q + 1) * CJ, :], AX.XY, ALU.max,
                                        apply_absolute_value=True).then_inc(rowmax_part, 1)

            def max_rows(t):
                dve.wait_ge(rowmax_part, CHUNKS * t + CHUNKS)
                nc.vector.tensor_reduce(rowmax[:, CHUNKS:CHUNKS + 1], rowmax[:, 0:CHUNKS], AX.X,
                                        ALU.max).then_inc(rowmax_ready, 1)

            def make_scale(t, first=False):
                dve.wait_ge(tabmax_ready, t + 1)
                if not first:
                    dve.wait_ge(coef_adopted, t)
                    dve.wait_ge(scaled, CHUNKS * t)
                ts = nc.vector.tensor_scalar
                ts(scale_tmp[:, 0:1], rowmax[:, CHUNKS + 1:CHUNKS + 2], TINY, None, ALU.max).then_inc(scale_step, 1)
                dve.wait_ge(scale_step, 2 * t + 1)
                ts(scale_tmp[:, 1:2].bitcast(I32), scale_tmp[:, 0:1].bitcast(I32), EXP_MASK, None,
                   ALU.bitwise_and).then_inc(scale_step, 1)
                dve.wait_ge(scale_step, 2 * t + 2)
                ts(coef_next[:, 0:1], scale_tmp[:, 1:2], COUNT_UNIT * 2.0 ** -HI_EXP, None, ALU.mult)
                ts(coef_next[:, 1:2], scale_tmp[:, 1:2], COUNT_UNIT * 2.0 ** -(HI_EXP + LO_SHIFT), None, ALU.mult)
                ts(coef_next[:, 2:3].bitcast(I32), scale_tmp[:, 1:2].bitcast(I32), -1.0,
                   float((2 * 127 + HI_EXP) * EXP_UNIT), ALU.mult, ALU.add).then_inc(scale_ready, 1)

            def adopt_coef(t, first=False):
                dve.wait_ge(scale_ready, t + 1)
                if not first:
                    dve.wait_ge(pooled_ready, BLOCKS * t)
                nc.vector.tensor_copy(coef[:, :], coef_next[:, 0:2]).then_inc(coef_adopted, 1)
                dve.wait_ge(coef_adopted, t + 1)

            tt = nc.vector.tensor_tensor

            def weight_columns(t, k, first=False):
                n = BLOCKS * t + k
                if not first:
                    dve.wait_ge(onehots_ready, PAIRS * n)
                whole = [GK, UNITS, COLS, UG]

                def by_unit(i):
                    return place[:, i, k * GROUPS:k * GROUPS + UNITS * UG].rearrange(
                        "p (u a g) -> p u a g", a=1, g=UG).to_broadcast(whole)

                iota = iota_by_unit[0:GK, 0:COLS, :].rearrange("p (a c) g -> p a c g", a=1).to_broadcast(whole)
                tt(weighted_c[:, :, :, :], iota, by_unit(1), ALU.is_equal).then_inc(weighted, 1)
                dve.wait_ge(weighted, 2 * n + 1)
                tt(weighted_c[:, :, :, :], weighted_c[:, :, :, :], by_unit(2), ALU.mult).then_inc(weighted, 1)
                dve.wait_ge(weighted, 2 * n + 2)

            def onehot_pair(t, k, d, first=False):
                if not (first and d < 2):
                    dve.wait_ge(unit_counted, UNITS * (BLOCKS * t + k) + 2 * d - 2)
                r = (PAIRS * k + d) % 2
                whole = [GK, 2, P, UG]
                g0 = k * GROUPS + 2 * UG * d
                at = place[:, 0, g0:g0 + 2 * UG].rearrange("p (u a g) -> p u a g", a=1, g=UG).to_broadcast(whole)
                iota = iota_by_unit[0:GK, :, :].rearrange("p (a c) g -> p a c g", a=1).to_broadcast(whole)
                tt(onehot_p[:, r, :, :, :], iota, at, ALU.is_equal)
                whole = [GK, 2 * COLS, GS, UG]
                cols = weighted_c[:, 2 * d:2 * d + 2, :, :].rearrange("p u (c a) g -> p (u c) a g", a=1).to_broadcast(whole)
                mask = sample_mask[0:GK, :, :].rearrange("p (a s) g -> p a s g", a=1).to_broadcast(whole)
                tt(onehot_c[:, r, :, :, :, :].rearrange("p u c s g -> p (u c) s g"), cols, mask,
                   ALU.mult).then_inc(onehots_ready, 1)

            def pool_bags(t, k, first=False):
                n = BLOCKS * t + k
                dve.wait_ge(block_summed, n + 1)
                nc.vector.tensor_scalar(lo_sum[:, :], acc[k % 2][D:2 * D, 0:NB], coef[D:2 * D, 1:2], None,
                                        ALU.mult).then_inc(lo_taken, 1)
                dve.wait_ge(lo_taken, n + 1)
                dve.wait_ge(pooled_free, n + 1)
                nc.vector.scalar_tensor_tensor(pooled[:, k % 2, :], acc[k % 2][0:D, 0:NB], coef[0:D, 0:1],
                                               lo_sum[:, :], ALU.mult, ALU.add).then_inc(pooled_ready, 1)
                dve.wait_ge(pooled_ready, n + 1)
                nc.vector.sem_inc(acc_free, 1)

            dve.wait_ge(consts_ready, 2)
            nc.vector.sem_inc(acc_free, 2)
            copy_indices(0, first=True)
            unturn(dve, turns, turned, unturned)
            for q in range(CHUNKS):
                max_chunk(0, q, first=True)
            max_rows(0)
            make_scale(0, first=True)
            adopt_coef(0, first=True)
            adopt_indices(0, first=True)
            weight_columns(0, 0, first=True)
            for d in range(PAIRS):
                onehot_pair(0, 0, d, first=True)
            AFTER = 1
            with dve.Fori(0, TP - 1) as t:
                weight_columns(t, 1)
                for d in range(PAIRS):
                    onehot_pair(t, 1, d)
                weight_columns(t, 2)
                for d in range(PAIRS):
                    onehot_pair(t, 2, d)
                    if d == AFTER:
                        pool_bags(t, 0)
                        copy_indices(t + 1)
                    if AFTER < d < AFTER + 1 + CHUNKS:
                        max_chunk(t + 1, d - AFTER - 1)
                    if d == AFTER + 1 + CHUNKS:
                        max_rows(t + 1)
                weight_columns(t, 3)
                for d in range(PAIRS):
                    onehot_pair(t, 3, d)
                    if d == AFTER:
                        pool_bags(t, 1)
                        make_scale(t + 1)
                adopt_indices(t + 1)
                weight_columns(t + 1, 0)
                for d in range(PAIRS):
                    onehot_pair(t + 1, 0, d)
                    if d == AFTER:
                        pool_bags(t, 2)
                pool_bags(t, 3)
                adopt_coef(t + 1)
            for k in range(1, BLOCKS):
                weight_columns(TP - 1, k)
                for d in range(PAIRS):
                    onehot_pair(TP - 1, k, d)
                    if d == AFTER and k >= 2:
                        pool_bags(TP - 1, k - 2)
            pool_bags(TP - 1, BLOCKS - 2)
            pool_bags(TP - 1, BLOCKS - 1)

            dve.wait_ge(block_summed, BLOCKS * TP)
            unturn(dve, top_turns, top_turned, top_unturned)
            for b in range(NGRAM):
                take_diagonals(dve, nc.vector.tensor_copy, b, (2, 3), diag_dve)


_INS = ["r_dense_x", "r_indices", "L0_rec_tables"] + [
    f"L0_rec_{x}_{part}{i}" for part in ("bot", "top") for i in range(3) for x in ("w", "b")]


def kernel(**inputs):
    import numpy as _np
    import concourse.bacc as _bacc
    from concourse import mybir as _mybir
    from concourse.bass_utils import run_bass_kernel_spmd as _run

    nc = _bacc.Bacc("TRN2", target_bir_lowering=False, num_devices=1, dynamic_dma_scratch_size=2048)
    arrays, args = {}, {}
    for name in _INS:
        a = _np.ascontiguousarray(inputs[name])
        arrays[f"in_{name}"] = a
        args[name] = nc.dram_tensor(f"in_{name}", a.shape, _mybir.dt.from_np(a.dtype), kind="ExternalInput").ap()
    B = args["r_dense_x"].shape[0]
    out = nc.dram_tensor("out", (B, 1), _mybir.dt.float32, kind="ExternalOutput").ap()

    def layers(x, part):
        return [args[f"L0_rec_{x}_{part}{i}"] for i in range(3)]

    build(nc, args["r_dense_x"], args["r_indices"], args["L0_rec_tables"], layers("w", "bot"), layers("b", "bot"),
          layers("w", "top"), layers("b", "top"), out)
    r = _run(nc, [arrays], core_ids=[0])
    return r.results[0]["out"]
```

```python
from contextlib import ExitStack

import concourse.bass as bass
from concourse import mybir

ALU = mybir.AluOpType
ACT = mybir.ActivationFunctionType
AX = mybir.AxisListType
F32 = mybir.dt.float32
F16 = mybir.dt.float16
BF16 = mybir.dt.bfloat16
I32 = mybir.dt.int32
U32 = mybir.dt.uint32
I16 = mybir.dt.int16
F8 = mybir.dt.float8e3

P = 128
QUAD = 32
BANK = 512

ROUND = 1.5 * 2.0 ** 23
HI_EXP = 14
LO_SHIFT = 11
COUNT_UNIT = 2.0 ** 6
EXP_UNIT = 2 ** 23
EXP_MASK = 0x7F800000
TINY = 2.0 ** -100


def build(nc, dense_x, indices, tables, w_bot, b_bot, w_top, b_top, out):
    T, B, L = indices.shape
    _, ROWS, D = tables.shape
    SLOTS = T + 1
    TG = 6
    TP = T - TG

    SPAN = -(-ROWS // P)
    COLS = -(-SPAN // 3)
    ABSENT = SPAN * P
    GS = P // L
    GK = GS * L
    GC = GS * COLS
    NB = BANK
    BLOCKS = B // NB
    GROUPS = -(-NB // GS)
    TAIL = NB - (GROUPS - 1) * GS
    UG = 4
    UNITS = -(-GROUPS // UG)
    PAIRS = UNITS // 2
    BPAD = GROUPS * GS
    CHUNKS = 7
    CJ = SPAN // CHUNKS
    HALF = (CHUNKS + 1) // 2
    assert B % NB == 0 and UNITS % 2 == 0 and BLOCKS % 2 == 0 and SPAN % CHUNKS == 0
    assert 2 * GC <= BANK and L < 32 and GROUPS <= P and 2 * D == P and SLOTS <= QUAD
    assert TP * ROWS + ABSENT <= T * ROWS
    BAG = P
    BAGS = B // BAG
    GB = 5
    GPAIRS = -(-GB // 2)
    LAST_BAGS = TG * BAGS - (TP - 1) * GB
    assert 0 < LAST_BAGS <= 2

    NBOT = [dense_x.shape[1]] + [w.shape[0] for w in w_bot]
    NTOP = [w_top[0].shape[1]] + [w.shape[0] for w in w_top]
    NF = NTOP[0]
    FCH = -(-NF // P)
    CHUNK_B = B // NB
    PAIR_ROW = [D + i * (i - 1) // 2 for i in range(SLOTS)]
    assert NF == PAIR_ROW[-1] + SLOTS - 1 and NTOP[3] == 1 and NBOT[3] == D

    rows_flat = tables.rearrange("t n d -> (t n) d")
    pooled_dram = nc.dram_tensor("pooled", [(TP + 1) * BLOCKS, D, NB], F32, kind="Internal").ap()
    gathered_dram = nc.dram_tensor("gathered", [GB + TG * BAGS, D, BAG], F32, kind="Internal").ap()

    def units_of(u):
        return range(u * UG, min((u + 1) * UG, GROUPS))

    ctx = ExitStack()
    with ctx:
        def sem(name):
            return ctx.enter_context(nc.semaphore(name))

        weights_in = sem("weights_in")
        consts_ready = sem("consts_ready")
        const_step = sem("const_step")
        turned = sem("turned")
        unturned = sem("unturned")
        bot_mm = sem("bot_mm")
        bot_act = sem("bot_act")
        bot_stored = sem("bot_stored")
        table_loaded = [sem(f"table_loaded{h}") for h in range(2)]
        idx_loaded = sem("idx_loaded")
        idx_converted = sem("idx_converted")
        idx_turned = sem("idx_turned")
        idx_copied = sem("idx_copied")
        idx_step = sem("idx_step")
        idx_ready = sem("idx_ready")
        idx_adopted = sem("idx_adopted")
        rowmax_part = sem("rowmax_part")
        rowmax_ready = sem("rowmax_ready")
        tabmax_ready = sem("tabmax_ready")
        scale_step = sem("scale_step")
        scale_ready = sem("scale_ready")
        coef_adopted = sem("coef_adopted")
        weighted = sem("weighted")
        hi_ready = sem("hi_ready")
        diff_ready = sem("diff_ready")
        parts_ready = sem("parts_ready")
        pool_waited = sem("pool_waited")
        chunk_used = sem("chunk_used")
        onehots_ready = sem("onehots_ready")
        unit_counted = sem("unit_counted")
        counts_ready = sem("counts_ready")
        block_summed = sem("block_summed")
        acc_free = sem("acc_free")
        lo_taken = sem("lo_taken")
        pooled_ready = sem("pooled_ready")
        pooled_stored = sem("pooled_stored")
        pooled_free = sem("pooled_free")
        look_loaded = sem("look_loaded")
        look_ready = sem("look_ready")
        look_free = sem("look_free")
        gathered = [sem(f"gathered{c}") for c in range(GB)]
        bags_ready = sem("bags_ready")
        bags_turned = sem("bags_turned")
        bags_copied = sem("bags_copied")
        bags_stored = sem("bags_stored")
        bags_free = sem("bags_free")
        slots_in = [sem(f"slots_in{i}") for i in range(2)]
        pads_zeroed = sem("pads_zeroed")
        dense_in = sem("dense_in")
        grams_ready = sem("grams_ready")
        diag_act = sem("diag_act")
        diag_dve = sem("diag_dve")
        top_in = sem("top_in")
        top_turned = sem("top_turned")
        top_unturned = sem("top_unturned")
        products_stored = sem("products_stored")
        pairs_in = [sem(f"pairs_in{r}") for r in range(NB // P)]
        top_mm = sem("top_mm")
        top_act = sem("top_act")
        out_stored = sem("out_stored")

        def sb(stack, name, shape, dt):
            return stack.enter_context(nc.sbuf_tensor(name, shape, dt))

        ident = sb(ctx, "ident", [P, P], F32)
        iota_by_unit = sb(ctx, "iota_by_unit", [P, P, UG], BF16)
        sample_mask = sb(ctx, "sample_mask", [P, GS, UG], BF16)
        sample_base = sb(ctx, "sample_base", [P, 1], F32)
        w_top2T = sb(ctx, "w_top2T", [P, NTOP[2] // P], F32)
        b_top0c = sb(ctx, "b_top0c", [P, NTOP[1] // P], F32)
        b_top1c = sb(ctx, "b_top1c", [P, NTOP[2] // P], F32)
        b_top2c = sb(ctx, "b_top2c", [1, 1], F32)
        idx_raw = sb(ctx, "idx_raw", [GROUPS, BLOCKS, GK], I32)

        early = ExitStack()
        sb(early, "even_counts", [P, COLS * BPAD + 8], F32)
        w_bot0r = sb(early, "w_bot0r", [P, NBOT[1] // P, NBOT[0]], F32)
        w_bot1r = sb(early, "w_bot1r", [P, NBOT[2] // P, NBOT[1]], F32)
        w_bot2r = sb(early, "w_bot2r", [D, NBOT[2]], F32)
        xr = sb(early, "xr", [P, B // P, NBOT[0]], F32)
        xT = sb(early, "xT", [NBOT[0], B], F32)
        w_bot0T = sb(early, "w_bot0T", [NBOT[0], NBOT[1]], F32)
        w_bot1T = sb(early, "w_bot1T", [P, NBOT[1] // P, NBOT[2]], F32)
        w_bot2T = sb(early, "w_bot2T", [P, NBOT[2] // P, D], F32)
        b_bot0c = sb(early, "b_bot0c", [P, NBOT[1] // P], F32)
        b_bot1c = sb(early, "b_bot1c", [P, NBOT[2] // P], F32)
        b_bot2c = sb(early, "b_bot2c", [D, 1], F32)
        h_bot0 = sb(early, "h_bot0", [P, 2, NBOT[1] // P, NB], F32)
        h_bot1 = sb(early, "h_bot1", [P, 2, NBOT[2] // P, NB], F32)
        x_bot = sb(early, "x_bot", [D, B], F32)
        iota_p = sb(early, "iota_p", [P, 1], F32)
        iota_s = sb(early, "iota_s", [P, GS, UG], BF16)
        early.close()

        loop = ExitStack()
        counts = [sb(loop, f"counts{i}", [P, COLS, BPAD], I32) for i in range(2)]
        count_bytes = [c[:, :, :].rearrange("p c b -> p (c b)").bitcast(F8).rearrange(
            "p (c b f) -> p c b f", b=BPAD, f=4) for c in counts]
        raw = sb(loop, "raw", [P, SPAN, D], F32)
        parts = sb(loop, "parts", [P, SPAN, 2 * D], F16)
        onehot_p = sb(loop, "onehot_p", [GK, 2, 2, P, UG], BF16)
        onehot_c = sb(loop, "onehot_c", [GK, 2, 2, COLS, GS, UG], BF16)
        weighted_c = sb(loop, "weighted_c", [GK, UNITS, COLS, UG], BF16)
        idx_f = sb(loop, "idx_f", [GROUPS, BLOCKS, GK], F32)
        NI = BLOCKS * GROUPS
        idx_t = sb(loop, "idx_t", [GK, NI], F32)
        scratch = sb(loop, "scratch", [GK, NI], F32)
        NIP = NI + UNITS * UG - GROUPS
        place_next = sb(loop, "place_next", [GK, 3, NIP], BF16)
        place = sb(loop, "place", [GK, 3, NIP], BF16)
        look = sb(loop, "look", [P, GB, L], I32)
        look_in = sb(loop, "look_in", [P, GB, L], I32)
        row_base = sb(loop, "row_base", [P, TG * BAGS], I32)
        bags = sb(loop, "bags", [P, GB, D], F32)
        bags_out = sb(loop, "bags_out", [P, 2 * GPAIRS, D], F32)
        bags_t = sb(loop, "bags_t", [P, GPAIRS, BAG], F32)
        rowmax = sb(loop, "rowmax", [P, CHUNKS + 2], F32)
        scale_tmp = sb(loop, "scale_tmp", [P, 4], F32)
        coef_next = sb(loop, "coef_next", [P, 3], F32)
        coef = sb(loop, "coef", [P, 2], F32)
        lo_sum = sb(loop, "lo_sum", [D, NB], F32)
        pooled = sb(loop, "pooled_sb", [D, 2, NB], F32)
        loop.close()

        late = ExitStack()
        HG = 64
        TILES = NB // (2 * HG)
        TB = CHUNK_B * 2 * HG
        assert 2 * HG == BAG and TILES == 4 and TB == NB
        slots = [sb(late, f"slots{i}", [P, CHUNK_B, QUAD, HG], F32) for i in range(2)]
        zt = sb(late, "zt", [P, SLOTS, NB], F32)
        y = sb(late, "y", [1, B], F32)
        ALIGN = 16
        over = 2 * COLS * BPAD - 2 * CHUNK_B * QUAD * HG - SLOTS * NB - B + ALIGN
        pad = sb(late, "pad", [P, over], F32)
        w_top0r = sb(late, "w_top0r", [P, NTOP[1] // P, NF], F32)
        w_top1r = sb(late, "w_top1r", [P, NTOP[2] // P, NTOP[1]], F32)
        w_top0T = sb(late, "w_top0T", [P, FCH, NTOP[1]], F32)
        w_top1T = sb(late, "w_top1T", [P, NTOP[1] // P, NTOP[2]], F32)
        assert over > 0 and 2 * CHUNK_B * QUAD * HG <= COLS * BPAD
        assert NTOP[1] // P * (NF + NTOP[2]) + NTOP[2] // P * NTOP[1] + FCH * NTOP[1] <= SPAN * D - ALIGN
        feats = sb(late, "feats", [P, FCH, B], F32)
        h_top0 = sb(late, "h_top0", [P, 2, NTOP[1] // P, TB], F32)
        h_top1 = sb(late, "h_top1", [P, 2, NTOP[2] // P, TB], F32)
        late.close()

        ps = ctx.enter_context(nc.psum_tensor("ps", [P, 8, BANK], F32))
        banks = [ps[:, i, :] for i in range(8)]
        unit_ps = [ps[:, 2 * i:2 * i + 2, :].rearrange("p b (h c) -> p (b h) c", h=2) for i in range(2)]
        acc = banks[4:6]
        idx_ps, bags_ps = banks[6], banks[7]
        bot_banks = [banks[4], banks[5], banks[7]]
        top_banks = banks[6:8]

        block = ctx.enter_context(nc.Block())

        turns = []
        for m in range(B // P):
            turns.append((xr[:, m, :], xT[:, m * P:(m + 1) * P]))
        for m in range(NBOT[1] // P):
            turns.append((w_bot0r[:, m, :], w_bot0T[:, m * P:(m + 1) * P]))
        for m in range(NBOT[2] // P):
            for k in range(NBOT[1] // P):
                turns.append((w_bot1r[:, m, k * P:(k + 1) * P], w_bot1T[:, k, m * P:(m + 1) * P]))
        for k in range(NBOT[2] // P):
            turns.append((w_bot2r[:, k * P:(k + 1) * P], w_bot2T[:, k, :]))
        top_turns = []
        for m in range(NTOP[1] // P):
            for k in range(FCH):
                n = min(P, NF - k * P)
                top_turns.append((w_top0r[:, m, k * P:k * P + n], w_top0T[0:n, k, m * P:(m + 1) * P]))
        for m in range(NTOP[2] // P):
            for k in range(NTOP[1] // P):
                top_turns.append((w_top1r[:, m, k * P:(k + 1) * P], w_top1T[:, k, m * P:(m + 1) * P]))

        weight_loads = [
            (xr[:, :, :], dense_x.rearrange("(m p) k -> p m k", p=P)),
            (w_bot0r[:, :, :], w_bot[0].rearrange("(m p) k -> p m k", p=P)),
            (w_bot1r[:, :, :], w_bot[1].rearrange("(m p) k -> p m k", p=P)),
            (w_bot2r[:, :], w_bot[2]),
            (b_bot0c[:, :], b_bot[0].rearrange("(m p) -> p m", p=P)),
            (b_bot1c[:, :], b_bot[1].rearrange("(m p) -> p m", p=P)),
            (b_bot2c[:, :], b_bot[2].rearrange("(m p) -> p m", p=D)),
        ]
        small_top_loads = [
            (w_top2T[:, :], w_top[2].rearrange("a (m p) -> p (a m)", p=P)),
            (b_top0c[:, :], b_top[0].rearrange("(m p) -> p m", p=P)),
            (b_top1c[:, :], b_top[1].rearrange("(m p) -> p m", p=P)),
            (b_top2c[:, :], b_top[2].rearrange("(m p) -> p m", p=1)),
        ]

        def layer(K, M, wT, src):
            for n in range(B // NB):
                for m in range(-(-M // P)):
                    mm = min(P, M - m * P)
                    terms = []
                    for k in range(-(-K // P)):
                        kk = min(P, K - k * P)
                        terms.append((wT(k, kk, m, mm), src(k, kk, n)))
                    yield m, mm, n, terms

        bot_layers = [
            list(layer(NBOT[0], NBOT[1], lambda k, kk, m, mm: w_bot0T[:, m * P:m * P + mm],
                       lambda k, kk, n: xT[:, n * NB:(n + 1) * NB])),
            list(layer(NBOT[1], NBOT[2], lambda k, kk, m, mm: w_bot1T[:, k, m * P:m * P + mm],
                       lambda k, kk, n: h_bot0[:, n % 2, k, :])),
            list(layer(NBOT[2], NBOT[3], lambda k, kk, m, mm: w_bot2T[:, k, :],
                       lambda k, kk, n: h_bot1[:, n % 2, k, :])),
        ]
        top_layers = [
            list(layer(NF, NTOP[1], lambda k, kk, m, mm: w_top0T[0:kk, k, m * P:m * P + mm],
                       lambda k, kk, n: feats[0:kk, k, n * NB:(n + 1) * NB])),
            list(layer(NTOP[1], NTOP[2], lambda k, kk, m, mm: w_top1T[:, k, m * P:m * P + mm],
                       lambda k, kk, n: h_top0[:, n % 2, k, :])),
            list(layer(NTOP[2], 1, lambda k, kk, m, mm: w_top2T[:, k:k + 1],
                       lambda k, kk, n: h_top1[:, n % 2, k, :])),
        ]
        bot_tiles, top_tiles = (sorted(((l, *t) for l, tiles in enumerate(layers) for t in tiles),
                                       key=lambda t: t[3]) for layers in (bot_layers, top_layers))
        LEAD = len(bot_tiles) - UNITS
        assert LEAD >= 0
        TOP_STEPS = len(top_tiles) // TILES

        def needed(tiles, i):
            l, n = tiles[i][0], tiles[i][3]
            done = [j for j, t in enumerate(tiles) if t[0] == l - 1 and t[3] == n]
            return done[-1] + 1 if done else 0

        def pieces(i):
            at, j = PAIR_ROW[i], 0
            while j < i:
                n = min(i - j, P - (at + j) % P)
                yield j, n, (at + j) // P, (at + j) % P
                j += n

        products_dram = nc.dram_tensor("products", [TILES, SLOTS, SLOTS, CHUNK_B, BAG], F32, kind="Internal").ap()
        NPIECE = sum(1 for i in range(1, SLOTS) for _ in pieces(i))
        GRAMS = 8
        NGRAM = NB // GRAMS
        GW = CHUNK_B * (SLOTS - 1)
        GRAMS_PER_TILE = NGRAM // TILES

        PER_UNIT = 4

        def take_diagonals(eng, copy, b, quarters, done):
            r, half, w = b // GRAMS_PER_TILE, b % 2, b % GRAMS_PER_TILE // 2
            g0 = r * 2 * HG + half * HG + GRAMS * w
            eng.wait_ge(grams_ready, b + 1)
            src = ps[:, 2 * (b % 3):2 * (b % 3) + 2, :].rearrange("p a (x c) -> p (a x) c", c=P)
            for k in quarters:
                rows = slice(QUAD * k, QUAD * (k + 1))
                last = copy(zt[rows, 1:, g0:g0 + GRAMS].rearrange("p s x -> p x s"),
                            src[rows, :, k * (SLOTS - 1):(k + 1) * (SLOTS - 1)])
            last.then_inc(done, 1)

        def turn(pe, items, full, out):
            for i, (src, dst) in enumerate(items):
                if i >= 4 * 4 and i % 4 == 0:
                    pe.wait_ge(out, i // 4 - 3)
                kp, m = src.shape[0], src.shape[1]
                last = nc.tensor.transpose(banks[i // 4 % 4][0:m, i % 4 * P:i % 4 * P + kp], src,
                                           ident[0:kp, 0:kp])
                if i % 4 == 3 or i == len(items) - 1:
                    last.then_inc(full, 1)
            pe.wait_ge(out, -(-len(items) // 4))

        def unturn(dve, items, full, out):
            for i, (src, dst) in enumerate(items):
                if i % 4 == 0:
                    dve.wait_ge(full, i // 4 + 1)
                kp, m = src.shape[0], src.shape[1]
                last = nc.vector.tensor_copy(dst, banks[i // 4 % 4][0:m, i % 4 * P:i % 4 * P + kp])
                if i % 4 == 3 or i == len(items) - 1:
                    last.then_inc(out, 1)

        @block.sync
        def _(sp):
            def load_table(src, h):
                j = slice(0, HALF * CJ) if h == 0 else slice(HALF * CJ, SPAN)
                sp.dma_start(raw[:, j, :], src.rearrange("(p j) d -> p j d", p=P)[:, j, :]
                             ).then_inc(table_loaded[h], 16)

            def load_indices(t):
                flat = indices[t].rearrange("b l -> (b l)").rearrange("(k r) -> k r", k=BLOCKS)
                cut = (GROUPS - 1) * GK
                sp.dma_start(idx_raw[0:GROUPS - 1, :, :],
                             flat[:, 0:cut].rearrange("k (g r) -> g k r", r=GK)).then_inc(idx_loaded, 16)
                sp.dma_start(idx_raw[GROUPS - 1:GROUPS, :, 0:TAIL * L],
                             flat[:, cut:NB * L].rearrange("k (g r) -> g k r", g=1)).then_inc(idx_loaded, 16)

            def load_lookups(n, bags=GB):
                sp.wait_ge(look_free, n + 1)
                flat = indices.rearrange("t b l -> (t b) l")
                sp.dma_start(look_in[:, 0:bags, :], flat[bass.ds(n * (GB * BAG) + TP * B, bags * BAG), :].rearrange(
                    "(c p) l -> p c l", p=BAG)).then_inc(look_loaded, 16)

            def store_pooled(t, k):
                sp.wait_ge(pooled_ready, BLOCKS * t + k + 1)
                sp.dma_start(pooled_dram[BLOCKS * t + BLOCKS + k], pooled[:, k % 2, :]).then_inc(pooled_stored, 16)
                sp.wait_ge(pooled_stored, 16 * (BLOCKS * t + k + 1))
                sp.sem_inc(pooled_free, 1)

            def store_bags(n, bags=GB):
                sp.wait_ge(bags_copied, n + 1)
                for h in range(2):
                    c = (bags - h + 1) // 2
                    if c:
                        dst = gathered_dram[bass.ds(n * GB + h, c, step=2), :, :] if c > 1 else \
                            gathered_dram[bass.ds(n * GB + h, 1), :, :]
                        sp.dma_start(dst.rearrange("c d b -> d c b"), bags_t[h * D:(h + 1) * D, 0:c, :]
                                     ).then_inc(bags_stored, 16)
                    else:
                        sp.sem_inc(bags_stored, 16)
                sp.wait_ge(bags_stored, 32 * n + 32)
                sp.sem_inc(bags_free, 1)

            sp.sem_inc(bags_free, 1)
            sp.sem_inc(pooled_free, 2)
            sp.wait_ge(const_step, 3)
            load_indices(0)
            with nc.allow_non_contiguous_dma(reason="small weights and biases"):
                for dst, src in weight_loads:
                    sp.dma_start(dst, src).then_inc(weights_in, 16)
                for h in range(2):
                    load_table(rows_flat[0:SPAN * P, :], h)
                for dst, src in small_top_loads:
                    sp.dma_start(dst, src).then_inc(top_in, 16)
            load_lookups(0)
            sp.wait_ge(idx_converted, 1)
            load_indices(1)

            def beside_table(t, last=False):
                sp.wait_ge(parts_ready, CHUNKS * t + CHUNKS)
                load_table(rows_flat[bass.ds((t + 1) * ROWS, SPAN * P), :], 0)
                store_pooled(t, 0)
                load_table(rows_flat[bass.ds((t + 1) * ROWS, SPAN * P), :], 1)
                store_pooled(t, 1)
                store_bags(t)
                store_pooled(t, 2)
                load_lookups(t + 1, LAST_BAGS if last else GB)
                if not last:
                    sp.wait_ge(idx_converted, t + 2)
                    load_indices(t + 2)
                store_pooled(t, 3)

            with sp.Fori(0, TP - 2) as t:
                beside_table(t)
            beside_table(TP - 2, last=True)
            sp.wait_ge(parts_ready, CHUNKS * TP)
            sp.dma_start(w_top0r[:, :, :], w_top[0].rearrange("(m p) k -> p m k", p=P)).then_inc(top_in, 16)
            sp.dma_start(w_top1r[:, :, :], w_top[1].rearrange("(m p) k -> p m k", p=P)).then_inc(top_in, 16)
            store_pooled(TP - 1, 0)
            store_pooled(TP - 1, 1)
            store_bags(TP - 1)

            def load_slots(r, blocks, s0, s1):
                for half in range(2):
                    g0 = r * 2 * HG + half * HG
                    for k in blocks:
                        sp.dma_start(slots[r % 2][half * D:(half + 1) * D, k, s0:s1, :],
                                     pooled_dram.rearrange("(s k) d g -> k d s g", k=BLOCKS)[
                                         k, :, s0:s1, g0:g0 + HG]).then_inc(slots_in[r % 2], 16)

            def load_gathered(r):
                for half in range(2):
                    for k in range(CHUNK_B):
                        sp.dma_start(slots[r % 2][half * D:(half + 1) * D, k, TP + 1:SLOTS, :],
                                     gathered_dram[GB:, :, :].rearrange(
                                         "(s k r) d g -> k r d s g", k=BLOCKS, s=TG)[
                                         k, r, :, :, half * HG:(half + 1) * HG]).then_inc(slots_in[r % 2], 16)

            def move_pairs(r):
                cols = slice(r * BAG, (r + 1) * BAG)
                sp.wait_ge(diag_act, GRAMS_PER_TILE * (r + 1))
                sp.wait_ge(diag_dve, GRAMS_PER_TILE * (r + 1))
                for k in range(CHUNK_B):
                    sp.dma_start(products_dram[r].rearrange("i j k g -> k j i g")[k, :, 1:, :],
                                 zt[QUAD * k:QUAD * k + SLOTS, 1:, cols]).then_inc(products_stored, 16)
                sp.wait_ge(products_stored, 16 * CHUNK_B * (r + 1))
                for i in range(1, SLOTS):
                    for j, n, ch, p0 in pieces(i):
                        sp.dma_start(feats[p0:p0 + n, ch, r * TB:(r + 1) * TB],
                                     products_dram[r, i, j:j + n, :, :].rearrange("j k g -> j (k g)")
                                     ).then_inc(pairs_in[r], 16)

            sp.wait_ge(block_summed, BLOCKS * TP - 1)
            load_slots(0, range(BLOCKS - 2), 0, TP + 1)
            store_pooled(TP - 1, BLOCKS - 2)
            load_slots(0, [BLOCKS - 2], 0, TP + 1)
            load_slots(0, [BLOCKS - 1], 0, TP)
            store_bags(TP, LAST_BAGS)
            load_gathered(0)
            store_pooled(TP - 1, BLOCKS - 1)
            load_slots(0, [BLOCKS - 1], TP, TP + 1)
            load_slots(1, range(BLOCKS), 0, TP + 1)
            load_gathered(1)
            for r in range(TILES):
                sp.dma_start(feats[0:D, 0, r * TB:(r + 1) * TB].rearrange("d (k g) -> d k g", k=BLOCKS),
                             pooled_dram[0:BLOCKS, :, r * BAG:(r + 1) * BAG].rearrange("k d g -> d k g")
                             ).then_inc(dense_in, 16)
            for r in range(TILES):
                if r + 2 < TILES:
                    sp.wait_ge(grams_ready, GRAMS_PER_TILE * (r + 1))
                    load_slots(r + 2, range(BLOCKS), 0, TP + 1)
                    load_gathered(r + 2)
                move_pairs(r)
            for r in range(TILES):
                sp.wait_ge(top_act, TOP_STEPS * (r + 1))
                sp.dma_start(out.rearrange("(k r g) a -> r a k g", k=BLOCKS, r=TILES)[r],
                             y[:, r * TB:(r + 1) * TB].rearrange("a (k g) -> a k g", k=BLOCKS)).then_inc(out_stored, 16)
            sp.wait_ge(out_stored, 16 * TILES)

        @block.gpsimd
        def _(pool):
            def await_alone(semaphore, value):
                pool.wait_ge(semaphore, value)
                pool.sem_inc(pool_waited, 1)

            nc.gpsimd.memset(ident[:, :], 0.0).then_inc(const_step, 1)
            nc.gpsimd.iota(iota_p[:, :], pattern=[[0, 1]], base=0, channel_multiplier=1,
                           allow_small_or_imprecise_dtypes=True).then_inc(const_step, 1)
            nc.gpsimd.memset(idx_raw[:, :, :], ABSENT).then_inc(const_step, 1)
            pool.wait_ge(const_step, 3)
            nc.gpsimd.affine_select(out=ident[:, :], in_=ident[:, :], compare_op=ALU.not_equal, fill=1.0,
                                    base=0, pattern=[[-1, P]], channel_multiplier=1).then_inc(consts_ready, 1)
            nc.gpsimd.iota(iota_by_unit[:, :, :], pattern=[[1, P], [0, UG]], base=0, channel_multiplier=0,
                           allow_small_or_imprecise_dtypes=True).then_inc(const_step, 1)
            nc.gpsimd.iota(iota_s[:, :, :], pattern=[[1, GS], [0, UG]], base=0, channel_multiplier=0,
                           allow_small_or_imprecise_dtypes=True).then_inc(const_step, 1)
            nc.gpsimd.iota(row_base[:, :], pattern=[[ROWS, TG], [0, BAGS]], base=TP * ROWS,
                           channel_multiplier=0).then_inc(const_step, 1)
            nc.gpsimd.memset(bags_out[:, :, :], 0.0).then_inc(bags_ready, 1)
            nc.gpsimd.memset(place_next[:, :, :], 0.0).then_inc(const_step, 1)
            nc.gpsimd.tensor_scalar(iota_p[:, :], iota_p[:, :], -(L - 1) / 2, 1.0 / L,
                                    ALU.add, ALU.mult).then_inc(const_step, 1)
            pool.wait_ge(const_step, 8)
            nc.gpsimd.tensor_scalar(sample_base[:, :], iota_p[:, :], ROUND, -ROUND,
                                    ALU.add, ALU.add).then_inc(const_step, 1)
            pool.wait_ge(const_step, 9)
            nc.gpsimd.tensor_scalar(sample_mask[:, :, :], iota_s[:, :, :], sample_base[:, :], None,
                                    ALU.is_equal).then_inc(consts_ready, 1)

            def convert_indices(t):
                await_alone(idx_loaded, 32 * t + 32)
                nc.gpsimd.tensor_copy(idx_f[:, :, :], idx_raw[:, :, :]).then_inc(idx_converted, 1)

            def table_max(t):
                await_alone(rowmax_ready, t + 1)
                nc.gpsimd.partition_all_reduce(rowmax[:, CHUNKS + 1:CHUNKS + 2], rowmax[:, CHUNKS:CHUNKS + 1], P,
                                               bass.bass_isa.ReduceOp.max).then_inc(tabmax_ready, 1)

            def make_lookups(n, bags=GB):
                await_alone(look_loaded, 16 * n + 16)
                nc.gpsimd.tensor_tensor(look[:, 0:bags, :], look_in[:, 0:bags, :],
                                        row_base[:, bass.ds(n * GB, bags)].to_broadcast([P, bags, L]),
                                        ALU.add).then_inc(look_ready, 1)
                await_alone(look_ready, n + 1)
                pool.sem_inc(look_free, 1)

            def gather(n, l, c):
                if l:
                    await_alone(gathered[c], 16 * (L * n + l))
                nc.gpsimd.indirect_dma_start(
                    bags[:, c, :], None, rows_flat,
                    bass.IndirectOffsetOnAxis(ap=look[:, c, l:l + 1].bitcast(U32), axis=0),
                    compute_op=ALU.add if l else ALU.bypass).then_inc(gathered[c], 16)

            def end_gathers(n, tiles=GB):
                for c in range(tiles):
                    pool.wait_ge(gathered[c], 16 * (L * n + L))
                await_alone(bags_turned, n + 1)
                nc.gpsimd.tensor_copy(bags_out[:, 0:tiles, :], bags[:, 0:tiles, :]).then_inc(bags_ready, 1)
                await_alone(bags_ready, n + 2)

            pool.sem_inc(look_free, 1)
            convert_indices(0)
            table_max(0)
            with pool.Fori(0, TP - 1) as t:
                make_lookups(t)
                for l in range(L):
                    for c in range(GB):
                        gather(t, l, c)
                    if l == 2:
                        convert_indices(t + 1)
                    elif l == 13:
                        table_max(t + 1)
                end_gathers(t)
            make_lookups(TP - 1, LAST_BAGS)
            for l in range(L):
                for c in range(LAST_BAGS):
                    gather(TP - 1, l, c)
            end_gathers(TP - 1, LAST_BAGS)
            pool.wait_ge(block_summed, BLOCKS * TP - 1)
            for q in range(2):
                nc.gpsimd.memset(slots[q][:, :, SLOTS:QUAD, :], 0.0).then_inc(pads_zeroed, 1)

        @block.tensor
        def _(pe):
            def mlp(tiles, into, mm_sem, act_sem, start=0, end=None):
                for i, (l, m, mm, n, terms) in list(enumerate(tiles))[start:end]:
                    ready = max(needed(tiles, i), i + 1 - len(into))
                    if ready > 0:
                        pe.wait_ge(act_sem, ready)
                    for k, (w, x) in enumerate(terms):
                        last = nc.tensor.matmul(into[i % len(into)][0:mm, :], w, x, start=(k == 0),
                                                stop=(k == len(terms) - 1))
                    last.then_inc(mm_sem, 1)

            def turn_indices(t, first=False):
                pe.wait_ge(idx_converted, t + 1)
                if not first:
                    pe.wait_ge(idx_copied, t)
                for k in range(BLOCKS):
                    last = nc.tensor.transpose(idx_ps[0:GK, k * GROUPS:(k + 1) * GROUPS], idx_f[:, k, :],
                                               ident[0:GROUPS, 0:GROUPS])
                last.then_inc(idx_turned, 1)

            def turn_bags(n):
                pe.wait_ge(bags_ready, n + 1)
                for q in range(GPAIRS):
                    last = nc.tensor.transpose(bags_ps[:, q * P:(q + 1) * P],
                                               bags_out[:, 2 * q:2 * q + 2, :].rearrange("p c d -> p (c d)"),
                                               ident[:, :])
                last.then_inc(bags_turned, 1)

            def count_unit(t, k, u, first=False):
                n = UNITS * (BLOCKS * t + k) + u
                if u % 2 == 0:
                    pe.wait_ge(onehots_ready, PAIRS * (BLOCKS * t + k) + u // 2 + 1)
                if not (first and u < 2):
                    pe.wait_ge(counts_ready, n - 1)
                r = (PAIRS * k + u // 2) % 2
                for g in units_of(u):
                    x = g % UG
                    last = nc.tensor.matmul(unit_ps[u % 2][:, x, 0:GC], onehot_p[:, r, u % 2, :, x],
                                            onehot_c[:, r, u % 2, :, :, x].rearrange("p c s -> p (c s)"),
                                            start=True, stop=True)
                last.then_inc(unit_counted, 1)

            def await_rows(t, k, j0, j1):
                n = BLOCKS * t + k
                if j0 == 0:
                    pe.wait_ge(counts_ready, UNITS * n + UNITS)
                    pe.wait_ge(acc_free, n + 1)
                for j in range(j0, j1):
                    if k == 0 and j % CJ == 0:
                        pe.wait_ge(parts_ready, CHUNKS * t + j // CJ + 1)

            def sum_rows(t, k, j):
                mm = nc.tensor.matmul(acc[k % 2][:, 0:NB], parts[:, j, :],
                                      count_bytes[k % 2][:, j % COLS, 0:NB, j // COLS],
                                      start=(j == 0), stop=(j == SPAN - 1))
                if j == SPAN - 1:
                    mm.then_inc(block_summed, 1)
                elif k == BLOCKS - 1 and j % CJ == CJ - 1:
                    mm.then_inc(chunk_used, 1)

            def phase(t, k, tn, kn):
                for u in range(UNITS):
                    j1 = SPAN if u == UNITS - 1 else PER_UNIT * (u + 1)
                    await_rows(t, k, PER_UNIT * u, j1)
                    count_unit(tn, kn, u)
                    for j in range(PER_UNIT * u, PER_UNIT * (u + 1)):
                        sum_rows(t, k, j)
                for j in range(PER_UNIT * UNITS, SPAN):
                    sum_rows(t, k, j)

            pe.wait_ge(consts_ready, 1)
            turn_indices(0, first=True)
            pe.wait_ge(weights_in, 16 * len(weight_loads))
            turn(pe, turns, turned, unturned)
            for i in range(len(bot_tiles)):
                mlp(bot_tiles, bot_banks, bot_mm, bot_act, i, i + 1)
                if i >= LEAD:
                    count_unit(0, 0, i - LEAD, first=True)
            pe.wait_ge(bot_act, len(bot_tiles))

            with pe.Fori(0, TP - 1) as t:
                phase(t, 0, t, 1)
                turn_indices(t + 1)
                phase(t, 1, t, 2)
                turn_bags(t)
                phase(t, 2, t, 3)
                phase(t, 3, t + 1, 0)
            for k in range(BLOCKS - 1):
                if k == 2:
                    turn_bags(TP - 1)
                phase(TP - 1, k, TP - 1, k + 1)
            await_rows(TP - 1, BLOCKS - 1, 0, SPAN)
            for j in range(SPAN):
                if j == SPAN // 2:
                    turn_bags(TP)
                sum_rows(TP - 1, BLOCKS - 1, j)

            pe.wait_ge(counts_ready, UNITS * BLOCKS * TP)
            pe.wait_ge(top_in, 16 * (len(small_top_loads) + 2))
            turn(pe, top_turns, top_turned, top_unturned)
            pe.wait_ge(acc_free, BLOCKS * TP + 2)
            pe.wait_ge(bags_copied, TP + 1)
            pe.wait_ge(pads_zeroed, 2)

            def make_grams(r):
                loads = 2 * 2 * CHUNK_B * (r // 2 + 1) + (2 if r % 2 == 0 else 0)
                pe.wait_ge(slots_in[r % 2], 16 * loads)
                for b in range(r * GRAMS_PER_TILE, (r + 1) * GRAMS_PER_TILE):
                    half, w = b % 2, b % GRAMS_PER_TILE // 2
                    if b >= 3:
                        pe.wait_ge(diag_act, b - 2)
                        pe.wait_ge(diag_dve, b - 2)
                    tile = slots[r % 2][half * D:(half + 1) * D, :, :, :].rearrange("p k s g -> p g k s")
                    for x in range(GRAMS):
                        g = GRAMS * w + x
                        last = nc.tensor.matmul(banks[2 * (b % 3) + x // 4][:, x % 4 * P:x % 4 * P + GW],
                                                tile[:, g, :, :].rearrange("p k s -> p (k s)"),
                                                tile[:, g, :, 1:SLOTS], start=True, stop=True)
                    last.then_inc(grams_ready, 1)

            def top_mlp(r):
                pe.wait_ge(dense_in, 16 * TILES)
                pe.wait_ge(pairs_in[r], 16 * NPIECE)
                mlp(top_tiles, top_banks, top_mm, top_act, TOP_STEPS * r, TOP_STEPS * (r + 1))

            make_grams(0)
            for r in range(1, TILES):
                make_grams(r)
                top_mlp(r - 1)
            top_mlp(TILES - 1)

        @block.scalar
        def _(act):
            def activated(l, m, n, outs, biases):
                cols = slice(n * NB, (n + 1) * NB)
                return (outs[l](m, n, cols) if l < 2 else outs[l][:, cols]), biases[l][:, m:m + 1]

            def make_hi(t, q, first=False):
                c = slice(q * CJ, (q + 1) * CJ)
                if q == 0:
                    act.wait_ge(scale_ready, t + 1)
                if not first and q < CHUNKS - 1:
                    act.wait_ge(chunk_used, (CHUNKS - 1) * (t - 1) + q + 1)
                nc.scalar.activation(parts[:, c, 0:D], raw[:, c, :], ACT.Copy,
                                     scale=coef_next[:, 2:3]).then_inc(hi_ready, 1)

            def make_lo(t, q):
                c = slice(q * CJ, (q + 1) * CJ)
                act.wait_ge(diff_ready, CHUNKS * t + q + 1)
                nc.scalar.activation(parts[:, c, D:2 * D], raw[:, c, :], ACT.Copy,
                                     scale=2.0 ** LO_SHIFT).then_inc(parts_ready, 1)

            def copy_bags(n):
                act.wait_ge(bags_turned, n + 1)
                act.wait_ge(bags_free, n + 1)
                nc.scalar.copy(bags_t[:, :, :], bags_ps[:, 0:GPAIRS * BAG].rearrange("p (q b) -> p q b", b=BAG)).then_inc(bags_copied, 1)

            def unpack_unit(t, k, u):
                n = UNITS * (BLOCKS * t + k) + u
                act.wait_ge(unit_counted, n + 1)
                g = len(units_of(u))
                nc.scalar.copy(
                    counts[k % 2][:, :, u * UG * GS:(u * UG + g) * GS].rearrange("p c (g s) -> p g c s", s=GS),
                    unit_ps[u % 2][:, 0:g, 0:GC].rearrange("p g (c s) -> p g c s", s=GS),
                ).then_inc(counts_ready, 1)

            for i, (l, m, mm, n, terms) in enumerate(bot_tiles):
                act.wait_ge(bot_mm, i + 1)
                dst, bias = activated(l, m, n, (lambda m, n, cols: h_bot0[:, n % 2, m, :],
                                               lambda m, n, cols: h_bot1[:, n % 2, m, :],
                                               x_bot), (b_bot0c, b_bot1c, b_bot2c))
                nc.scalar.activation(dst, bot_banks[i % 3][0:mm, :], ACT.Relu, bias=bias).then_inc(bot_act, 1)
                if i >= LEAD:
                    unpack_unit(0, 0, i - LEAD)
                if LEAD < i <= LEAD + CHUNKS - 1:
                    make_hi(0, i - LEAD - 1, first=True)
                if i in range(LEAD + 6, LEAD + 6 + 2 * (CHUNKS - 3), 2):
                    make_lo(0, (i - LEAD - 6) // 2)
            act.wait_ge(bot_act, len(bot_tiles))
            act.dma_start(pooled_dram[0:BLOCKS, :, :].rearrange("k d g -> d k g"),
                          x_bot[:, :].rearrange("d (k g) -> d k g", k=BLOCKS)).then_inc(bot_stored, 16)
            act.wait_ge(bot_stored, 16)
            AHEAD = 2
            for u in range(AHEAD):
                unpack_unit(0, 1, u)
            hi_after = {-(-CJ * (q + 1) // PER_UNIT) + 1: q for q in range(CHUNKS - 2)}
            lo_after = {u + 4: q for u, q in hi_after.items() if u + 4 < UNITS}
            assert len(lo_after) == CHUNKS - 3

            def unpack_block1(t):
                for u in range(AHEAD, UNITS):
                    unpack_unit(t, 1, u)
                    if u == AHEAD:
                        make_hi(t, CHUNKS - 1)
                    elif u in (4, 6, 8):
                        make_lo(t, CHUNKS - 3 + (u - 4) // 2)

            with act.Fori(0, TP - 1) as t:
                unpack_block1(t)
                for k in range(2, BLOCKS):
                    for u in range(UNITS):
                        unpack_unit(t, k, u)
                        if k == BLOCKS - 1 and u == 3:
                            copy_bags(t)
                for u in range(UNITS):
                    unpack_unit(t + 1, 0, u)
                    if u in hi_after:
                        make_hi(t + 1, hi_after[u])
                    if u in lo_after:
                        make_lo(t + 1, lo_after[u])
                unpack_unit(t + 1, 1, 0)
                make_hi(t + 1, CHUNKS - 2)
                unpack_unit(t + 1, 1, 1)
            unpack_block1(TP - 1)
            for k in range(2, BLOCKS):
                for u in range(UNITS):
                    unpack_unit(TP - 1, k, u)
                    if k == BLOCKS - 1 and u == 3:
                        copy_bags(TP - 1)
            copy_bags(TP)

            act.wait_ge(block_summed, BLOCKS * TP)

            def diagonals(r):
                for b in range(r * GRAMS_PER_TILE, (r + 1) * GRAMS_PER_TILE):
                    take_diagonals(act, nc.scalar.copy, b, (0, 1), diag_act)

            def top_activations(r):
                for i in range(TOP_STEPS * r, TOP_STEPS * (r + 1)):
                    l, m, mm, n, terms = top_tiles[i]
                    act.wait_ge(top_mm, i + 1)
                    dst, bias = activated(l, m, n, (lambda m, n, cols: h_top0[:, n % 2, m, :],
                                                    lambda m, n, cols: h_top1[:, n % 2, m, :],
                                                    y), (b_top0c, b_top1c, b_top2c))
                    nc.scalar.activation(dst, top_banks[i % 2][0:mm, :], ACT.Sigmoid if l == 2 else ACT.Relu,
                                         bias=bias).then_inc(top_act, 1)

            diagonals(0)
            for r in range(1, TILES):
                diagonals(r)
                top_activations(r - 1)
            top_activations(TILES - 1)

        @block.vector
        def _(dve):
            def copy_indices(t, first=False):
                dve.wait_ge(idx_turned, t + 1)
                if not first:
                    dve.wait_ge(idx_ready, t)
                nc.vector.tensor_copy(idx_t[:, :], idx_ps[0:GK, 0:NI]).then_inc(idx_copied, 1)

            ts = nc.vector.tensor_scalar
            part_i, col_i, weight_i = (place_next[:, i, 0:NI] for i in range(3))
            IDX_STEPS = 8

            def find_partition(t):
                dve.wait_ge(idx_copied, t + 1)
                ts(scratch[:, :], idx_t[:, :], -(SPAN - 1) / 2, 1.0 / SPAN, ALU.add, ALU.mult).then_inc(idx_step, 1)
                dve.wait_ge(idx_step, IDX_STEPS * t + 1)
                ts(part_i, scratch[:, :], ROUND, -ROUND, ALU.add, ALU.add).then_inc(idx_step, 1)
                dve.wait_ge(idx_step, IDX_STEPS * t + 2)
                ts(scratch[:, :], part_i, -float(SPAN), 0.0, ALU.mult, ALU.add).then_inc(idx_step, 1)
                dve.wait_ge(idx_step, IDX_STEPS * t + 3)
                nc.vector.tensor_tensor(idx_t[:, :], idx_t[:, :], scratch[:, :], ALU.add).then_inc(idx_step, 1)

            def find_field(t):
                dve.wait_ge(idx_step, IDX_STEPS * t + 4)
                ts(scratch[:, :], idx_t[:, :], -(COLS - 1) / 2, 1.0 / COLS, ALU.add, ALU.mult).then_inc(idx_step, 1)
                dve.wait_ge(idx_step, IDX_STEPS * t + 5)
                ts(scratch[:, :], scratch[:, :], ROUND, -ROUND, ALU.add, ALU.add).then_inc(idx_step, 1)

            def find_column(t):
                dve.wait_ge(idx_step, IDX_STEPS * t + 6)
                ts(weight_i.bitcast(I16), scratch[:, :], 8.0 * 128, 127.0 * 128, ALU.mult,
                   ALU.add).then_inc(idx_step, 1)
                dve.wait_ge(idx_step, IDX_STEPS * t + 7)
                ts(scratch[:, :], scratch[:, :], -float(COLS), 0.0, ALU.mult, ALU.add).then_inc(idx_step, 1)
                dve.wait_ge(idx_step, IDX_STEPS * t + 8)
                nc.vector.tensor_tensor(col_i, idx_t[:, :], scratch[:, :], ALU.add).then_inc(idx_ready, 1)

            def adopt_indices(t, first=False):
                dve.wait_ge(idx_ready, t + 1)
                if not first:
                    dve.wait_ge(onehots_ready, PAIRS * BLOCKS * t)
                nc.vector.tensor_copy(place[:, :, :], place_next[:, :, :]).then_inc(idx_adopted, 1)
                dve.wait_ge(idx_adopted, t + 1)

            def max_chunk(t, q, first=False):
                if q in (0, HALF):
                    dve.wait_ge(table_loaded[q // HALF], 16 * t + 16)
                if q == 0 and not first:
                    dve.wait_ge(tabmax_ready, t)
                nc.vector.tensor_reduce(rowmax[:, q:q + 1], raw[:, q * CJ:(q + 1) * CJ, :], AX.XY, ALU.max,
                                        apply_absolute_value=True).then_inc(rowmax_part, 1)

            def max_rows(t):
                dve.wait_ge(rowmax_part, CHUNKS * t + CHUNKS)
                nc.vector.tensor_reduce(rowmax[:, CHUNKS:CHUNKS + 1], rowmax[:, 0:CHUNKS], AX.X,
                                        ALU.max).then_inc(rowmax_ready, 1)

            def make_scale(t, first=False):
                dve.wait_ge(tabmax_ready, t + 1)
                if not first:
                    dve.wait_ge(coef_adopted, t)
                    dve.wait_ge(diff_ready, CHUNKS * t)
                ts(scale_tmp[:, 0:1], rowmax[:, CHUNKS + 1:CHUNKS + 2], TINY, None, ALU.max).then_inc(scale_step, 1)
                dve.wait_ge(scale_step, 2 * t + 1)
                ts(scale_tmp[:, 1:2].bitcast(I32), scale_tmp[:, 0:1].bitcast(I32), EXP_MASK, None,
                   ALU.bitwise_and).then_inc(scale_step, 1)
                dve.wait_ge(scale_step, 2 * t + 2)
                ts(coef_next[:, 0:1], scale_tmp[:, 1:2], COUNT_UNIT * 2.0 ** -HI_EXP, None, ALU.mult)
                ts(coef_next[:, 1:2], scale_tmp[:, 1:2], COUNT_UNIT * 2.0 ** -(HI_EXP + LO_SHIFT), None, ALU.mult)
                ts(coef_next[:, 2:3].bitcast(I32), scale_tmp[:, 1:2].bitcast(I32), -1.0,
                   float((2 * 127 + HI_EXP) * EXP_UNIT), ALU.mult, ALU.add).then_inc(scale_ready, 1)

            def subtract_hi(t, q):
                c = slice(q * CJ, (q + 1) * CJ)
                dve.wait_ge(hi_ready, CHUNKS * t + q + 1)
                nc.vector.scalar_tensor_tensor(raw[:, c, :], raw[:, c, :], coef_next[:, 2:3], parts[:, c, 0:D],
                                               ALU.mult, ALU.subtract).then_inc(diff_ready, 1)

            def adopt_coef(t, first=False):
                dve.wait_ge(scale_ready, t + 1)
                if not first:
                    dve.wait_ge(pooled_ready, BLOCKS * t)
                nc.vector.tensor_copy(coef[:, :], coef_next[:, 0:2]).then_inc(coef_adopted, 1)
                dve.wait_ge(coef_adopted, t + 1)

            tt = nc.vector.tensor_tensor

            def weight_columns(t, k, first=False):
                n = BLOCKS * t + k
                if not first:
                    dve.wait_ge(onehots_ready, PAIRS * n)
                whole = [GK, UNITS, COLS, UG]

                def by_unit(i):
                    return place[:, i, k * GROUPS:k * GROUPS + UNITS * UG].rearrange(
                        "p (u a g) -> p u a g", a=1, g=UG).to_broadcast(whole)

                iota = iota_by_unit[0:GK, 0:COLS, :].rearrange("p (a c) g -> p a c g", a=1).to_broadcast(whole)
                tt(weighted_c[:, :, :, :], iota, by_unit(1), ALU.is_equal).then_inc(weighted, 1)
                dve.wait_ge(weighted, 2 * n + 1)
                tt(weighted_c[:, :, :, :], weighted_c[:, :, :, :], by_unit(2), ALU.mult).then_inc(weighted, 1)
                dve.wait_ge(weighted, 2 * n + 2)

            def onehot_pair(t, k, d, first=False):
                if not (first and d < 2):
                    dve.wait_ge(unit_counted, UNITS * (BLOCKS * t + k) + 2 * d - 2)
                r = (PAIRS * k + d) % 2
                whole = [GK, 2, P, UG]
                g0 = k * GROUPS + 2 * UG * d
                at = place[:, 0, g0:g0 + 2 * UG].rearrange("p (u a g) -> p u a g", a=1, g=UG).to_broadcast(whole)
                iota = iota_by_unit[0:GK, :, :].rearrange("p (a c) g -> p a c g", a=1).to_broadcast(whole)
                tt(onehot_p[:, r, :, :, :], iota, at, ALU.is_equal)
                whole = [GK, 2 * COLS, GS, UG]
                cols = weighted_c[:, 2 * d:2 * d + 2, :, :].rearrange("p u (c a) g -> p (u c) a g", a=1).to_broadcast(whole)
                mask = sample_mask[0:GK, :, :].rearrange("p (a s) g -> p a s g", a=1).to_broadcast(whole)
                tt(onehot_c[:, r, :, :, :, :].rearrange("p u c s g -> p (u c) s g"), cols, mask,
                   ALU.mult).then_inc(onehots_ready, 1)

            def pool_bags(t, k):
                n = BLOCKS * t + k
                dve.wait_ge(block_summed, n + 1)
                nc.vector.tensor_scalar(lo_sum[:, :], acc[k % 2][D:2 * D, 0:NB], coef[D:2 * D, 1:2], None,
                                        ALU.mult).then_inc(lo_taken, 1)
                dve.wait_ge(lo_taken, n + 1)
                dve.wait_ge(pooled_free, n + 1)
                nc.vector.scalar_tensor_tensor(pooled[:, k % 2, :], acc[k % 2][0:D, 0:NB], coef[0:D, 0:1],
                                               lo_sum[:, :], ALU.mult, ALU.add).then_inc(pooled_ready, 1)
                dve.wait_ge(pooled_ready, n + 1)
                nc.vector.sem_inc(acc_free, 1)

            dve.wait_ge(consts_ready, 2)
            nc.vector.sem_inc(acc_free, 2)
            copy_indices(0, first=True)
            find_partition(0)
            find_field(0)
            find_column(0)
            adopt_indices(0, first=True)
            unturn(dve, turns, turned, unturned)
            for q in range(CHUNKS):
                max_chunk(0, q, first=True)
            max_rows(0)
            weight_columns(0, 0, first=True)
            onehot_pair(0, 0, 0, first=True)
            onehot_pair(0, 0, 1, first=True)
            make_scale(0, first=True)
            adopt_coef(0, first=True)
            for d in range(2, PAIRS):
                onehot_pair(0, 0, d, first=True)
                if d - 2 < CHUNKS - 3:
                    subtract_hi(0, d - 2)
            AHEAD = 2
            weight_columns(0, 1)
            for d in range(AHEAD):
                onehot_pair(0, 1, d)

            def onehots_block1(t):
                for d in range(AHEAD, PAIRS):
                    onehot_pair(t, 1, d)
                    if d < AHEAD + 3:
                        subtract_hi(t, CHUNKS - 3 + d - AHEAD)

            with dve.Fori(0, TP - 1) as t:
                onehots_block1(t)
                weight_columns(t, 2)
                for d in range(PAIRS):
                    onehot_pair(t, 2, d)
                    if d == 1:
                        pool_bags(t, 0)
                    elif d == 2:
                        copy_indices(t + 1)
                    elif d == 3:
                        find_partition(t + 1)
                    elif d == 5:
                        find_field(t + 1)
                    elif 7 <= d <= 9:
                        max_chunk(t + 1, d - 7)
                weight_columns(t, 3)
                for d in range(PAIRS):
                    onehot_pair(t, 3, d)
                    if d == 1:
                        pool_bags(t, 1)
                    elif 2 <= d <= 5:
                        max_chunk(t + 1, d + 1)
                        if d == 5:
                            max_rows(t + 1)
                    elif d == 7:
                        find_column(t + 1)
                    elif d == 9:
                        make_scale(t + 1)
                adopt_indices(t + 1)
                weight_columns(t + 1, 0)
                for d in range(PAIRS):
                    onehot_pair(t + 1, 0, d)
                    if d == 1:
                        pool_bags(t, 2)
                    elif d in (4, 6, 8, 10):
                        subtract_hi(t + 1, (d - 4) // 2)
                weight_columns(t + 1, 1)
                for d in range(AHEAD):
                    onehot_pair(t + 1, 1, d)
                pool_bags(t, 3)
                adopt_coef(t + 1)
            onehots_block1(TP - 1)
            for k in range(2, BLOCKS):
                weight_columns(TP - 1, k)
                for d in range(PAIRS):
                    onehot_pair(TP - 1, k, d)
                    if d == 1:
                        pool_bags(TP - 1, k - 2)
            pool_bags(TP - 1, BLOCKS - 2)
            pool_bags(TP - 1, BLOCKS - 1)

            unturn(dve, top_turns, top_turned, top_unturned)
            for b in range(NGRAM):
                take_diagonals(dve, nc.vector.tensor_copy, b, (2, 3), diag_dve)


_INS = ["r_dense_x", "r_indices", "L0_rec_tables"] + [
    f"L0_rec_{x}_{part}{i}" for part in ("bot", "top") for i in range(3) for x in ("w", "b")]


def kernel(**inputs):
    import numpy as _np
    import concourse.bacc as _bacc
    from concourse import mybir as _mybir
    from concourse.bass_utils import run_bass_kernel_spmd as _run

    nc = _bacc.Bacc("TRN2", target_bir_lowering=False, num_devices=1, dynamic_dma_scratch_size=2048)
    arrays, args = {}, {}
    for name in _INS:
        a = _np.ascontiguousarray(inputs[name])
        arrays[f"in_{name}"] = a
        args[name] = nc.dram_tensor(f"in_{name}", a.shape, _mybir.dt.from_np(a.dtype), kind="ExternalInput").ap()
    B = args["r_dense_x"].shape[0]
    out = nc.dram_tensor("out", (B, 1), _mybir.dt.float32, kind="ExternalOutput").ap()

    def layers(x, part):
        return [args[f"L0_rec_{x}_{part}{i}"] for i in range(3)]

    build(nc, args["r_dense_x"], args["r_indices"], args["L0_rec_tables"], layers("w", "bot"), layers("b", "bot"),
          layers("w", "top"), layers("b", "top"), out)
    r = _run(nc, [arrays], core_ids=[0])
    return r.results[0]["out"]
```
